# Optimizing a Trainium2 kernel written in Bass

```python
import numpy as np
import jax
import jax.numpy as jnp

def _softmax(x, axis=-1):
    return jax.nn.softmax(x, axis=axis)

def _gelu(x):
    return jax.nn.gelu(x, approximate=True)

def _silu(x):
    return jax.nn.silu(x)

def _sigmoid(x):
    return jax.nn.sigmoid(x)

def _layernorm(x, axis=-1, eps=1e-05):
    m = jnp.mean(x, axis=axis, keepdims=True)
    v = jnp.var(x, axis=axis, keepdims=True)
    return (x - m) / jnp.sqrt(v + eps)

def _scatter_add(tgt, idx, src, axis=0):
    return tgt.at[idx].add(src)

def _segment_sum(src, seg, n):
    return jax.ops.segment_sum(src, seg, n)
kernel_name = 'mk_prb_d1_jaxref_r4_7a048c'

def setup_inputs(seed: int=0):
    np.random.seed(seed)
    _w = jnp.asarray

    def _L0_attn_setup():
        import jax, jax.numpy as jnp
        import numpy as np
        B, S, D = (2, 512, 256)
        H, DH = (16, 64)
        DQL, DKVL = (128, 128)
        DR = 64
        TOPK = 64
        LN_EPS = 1e-05
        ROPE_BASE = 10000.0

        def _rope_tables(seq_len, dim):
            inv_freq = 1.0 / ROPE_BASE ** (np.arange(0, dim, 2, dtype=np.float32) / dim)
            t = np.arange(seq_len, dtype=np.float32)
            freqs = np.outer(t, inv_freq)
            cos = np.concatenate([np.cos(freqs), np.cos(freqs)], -1)[:, ::2]
            sin = np.concatenate([np.sin(freqs), np.sin(freqs)], -1)[:, ::2]
            return (jnp.asarray(cos), jnp.asarray(sin))

        def _apply_rope_subspace(x, d_rope):
            s = x.shape[-2]
            cos, sin = _rope_tables(s, d_rope)
            xr, xp = (x[..., :d_rope], x[..., d_rope:])
            e, o = (xr[..., 0::2], xr[..., 1::2])
            rot = jnp.stack([e * cos - o * sin, e * sin + o * cos], axis=-1).reshape(xr.shape)
            return jnp.concatenate([rot, xp], axis=-1)

        def _reference_tuple_inner(x, w_down_q, w_down_kv, w_up_q, w_up_k, w_up_v, w_out, ln_scale, ln_bias):
            b, s, d = x.shape
            residual = x
            mu = jnp.mean(x, axis=-1, keepdims=True)
            var = jnp.mean((x - mu) ** 2, axis=-1, keepdims=True)
            h = (x - mu) * jax.lax.rsqrt(var + LN_EPS) * ln_scale + ln_bias
            c_q = h @ w_down_q.T
            c_kv = h @ w_down_kv.T
            q = (c_q @ w_up_q.T).reshape(b, s, H, DH).transpose(0, 2, 1, 3)
            k = (c_kv @ w_up_k.T).reshape(b, s, H, DH).transpose(0, 2, 1, 3)
            v = (c_kv @ w_up_v.T).reshape(b, s, H, DH).transpose(0, 2, 1, 3)
            q = _apply_rope_subspace(q, DR)
            k = _apply_rope_subspace(k, DR)
            scale = 1.0 / np.sqrt(DH).astype(np.float32)
            scores = jnp.einsum('bhqd,bhkd->bhqk', q, k) * scale
            _, indices = jax.lax.top_k(scores, min(TOPK, s))
            attn = jax.nn.softmax(scores, axis=-1)
            out = jnp.einsum('bhqk,bhkd->bhqd', attn, v)
            out = out.transpose(0, 2, 1, 3).reshape(b, s, H * DH)
            out = out @ w_out.T + residual
            return (out, indices.astype(jnp.int64))
        key = jax.random.key(seed)
        ks = jax.random.split(key, 7)
        init = lambda k, shape: jax.random.normal(k, shape, jnp.float32) * 0.02
        return {'x': jax.random.normal(ks[0], (B, S, D), jnp.float32), 'w_down_q': init(ks[1], (DQL, D)), 'w_down_kv': init(ks[2], (DKVL, D)), 'w_up_q': init(ks[3], (H * DH, DQL)), 'w_up_k': init(ks[4], (H * DH, DKVL)), 'w_up_v': init(ks[5], (H * DH, DKVL)), 'w_out': init(ks[6], (D, H * DH)), 'ln_scale': jnp.ones((D,), jnp.float32), 'ln_bias': jnp.zeros((D,), jnp.float32)}
    _L0_attn_in = _L0_attn_setup()

    def _L0_ffn_setup():
        import jax, jax.numpy as jnp
        import numpy as np
        LN_EPS = 1e-05

        def layer_norm(x, g, b):
            mu = jnp.mean(x, axis=-1, keepdims=True)
            var = jnp.var(x, axis=-1, keepdims=True)
            return (x - mu) / jnp.sqrt(var + LN_EPS) * g + b

        def balanced_assignment(scores):
            T, E = scores.shape
            C = T // E
            taken = jnp.zeros((T,), dtype=bool)
            parts = []
            for e in range(E):
                s = jnp.where(taken, -jnp.inf, scores[:, e])
                _, idx = jax.lax.top_k(s, C)
                parts.append(idx)
                taken = taken.at[idx].set(True)
            return jnp.concatenate(parts)
        key = jax.random.key(seed)
        ks = jax.random.split(key, 4)
        B, S, D, F, E = (4, 512, 256, 1024, 8)
        return {'x': jax.random.normal(ks[0], (B, S, D), dtype=jnp.float32), 'centroids': jax.random.normal(ks[1], (E, D), dtype=jnp.float32) * 0.1, 'ln_g': jnp.ones((D,), dtype=jnp.float32), 'ln_b': jnp.zeros((D,), dtype=jnp.float32), 'w1': jax.random.normal(ks[2], (E, D, F), dtype=jnp.float32) * 0.02, 'b1': jnp.zeros((E, F), dtype=jnp.float32), 'w2': jax.random.normal(ks[3], (E, F, D), dtype=jnp.float32) * 0.02, 'b2': jnp.zeros((E, D), dtype=jnp.float32)}
    _L0_ffn_in = _L0_ffn_setup()
    _d = {'L0_attn_x': _L0_attn_in['x'], 'L0_attn_w_down_q': _L0_attn_in['w_down_q'], 'L0_attn_w_down_kv': _L0_attn_in['w_down_kv'], 'L0_attn_w_up_q': _L0_attn_in['w_up_q'], 'L0_attn_w_up_k': _L0_attn_in['w_up_k'], 'L0_attn_w_up_v': _L0_attn_in['w_up_v'], 'L0_attn_w_out': _L0_attn_in['w_out'], 'L0_attn_ln_scale': _L0_attn_in['ln_scale'], 'L0_attn_ln_bias': _L0_attn_in['ln_bias'], 'L0_ffn_centroids': _L0_ffn_in['centroids'], 'L0_ffn_ln_g': _L0_ffn_in['ln_g'], 'L0_ffn_ln_b': _L0_ffn_in['ln_b'], 'L0_ffn_w1': _L0_ffn_in['w1'], 'L0_ffn_b1': _L0_ffn_in['b1'], 'L0_ffn_w2': _L0_ffn_in['w2'], 'L0_ffn_b2': _L0_ffn_in['b2']}
    _x0 = _d['L0_attn_x']
    _d['L0_attn_x'] = jax.random.normal(jax.random.fold_in(jax.random.key(seed), 1), (16, 512, 256), dtype=_x0.dtype)
    del _x0
    return _d

def reference(L0_attn_x, L0_attn_w_down_q, L0_attn_w_down_kv, L0_attn_w_up_q, L0_attn_w_up_k, L0_attn_w_up_v, L0_attn_w_out, L0_attn_ln_scale, L0_attn_ln_bias, L0_ffn_centroids, L0_ffn_ln_g, L0_ffn_ln_b, L0_ffn_w1, L0_ffn_b1, L0_ffn_w2, L0_ffn_b2):

    def _L0_attn_ref(x, w_down_q, w_down_kv, w_up_q, w_up_k, w_up_v, w_out, ln_scale, ln_bias):
        import jax, jax.numpy as jnp
        import numpy as np
        B, S, D = (2, 512, 256)
        H, DH = (16, 64)
        DQL, DKVL = (128, 128)
        DR = 64
        TOPK = 64
        LN_EPS = 1e-05
        ROPE_BASE = 10000.0

        def _rope_tables(seq_len, dim):
            inv_freq = 1.0 / ROPE_BASE ** (np.arange(0, dim, 2, dtype=np.float32) / dim)
            t = np.arange(seq_len, dtype=np.float32)
            freqs = np.outer(t, inv_freq)
            cos = np.concatenate([np.cos(freqs), np.cos(freqs)], -1)[:, ::2]
            sin = np.concatenate([np.sin(freqs), np.sin(freqs)], -1)[:, ::2]
            return (jnp.asarray(cos), jnp.asarray(sin))

        def _apply_rope_subspace(x, d_rope):
            s = x.shape[-2]
            cos, sin = _rope_tables(s, d_rope)
            xr, xp = (x[..., :d_rope], x[..., d_rope:])
            e, o = (xr[..., 0::2], xr[..., 1::2])
            rot = jnp.stack([e * cos - o * sin, e * sin + o * cos], axis=-1).reshape(xr.shape)
            return jnp.concatenate([rot, xp], axis=-1)

        def _reference_tuple_inner(x, w_down_q, w_down_kv, w_up_q, w_up_k, w_up_v, w_out, ln_scale, ln_bias):
            b, s, d = x.shape
            residual = x
            mu = jnp.mean(x, axis=-1, keepdims=True)
            var = jnp.mean((x - mu) ** 2, axis=-1, keepdims=True)
            h = (x - mu) * jax.lax.rsqrt(var + LN_EPS) * ln_scale + ln_bias
            c_q = h @ w_down_q.T
            c_kv = h @ w_down_kv.T
            q = (c_q @ w_up_q.T).reshape(b, s, H, DH).transpose(0, 2, 1, 3)
            k = (c_kv @ w_up_k.T).reshape(b, s, H, DH).transpose(0, 2, 1, 3)
            v = (c_kv @ w_up_v.T).reshape(b, s, H, DH).transpose(0, 2, 1, 3)
            q = _apply_rope_subspace(q, DR)
            k = _apply_rope_subspace(k, DR)
            scale = 1.0 / np.sqrt(DH).astype(np.float32)
            scores = jnp.einsum('bhqd,bhkd->bhqk', q, k) * scale
            _, indices = jax.lax.top_k(scores, min(TOPK, s))
            attn = jax.nn.softmax(scores, axis=-1)
            out = jnp.einsum('bhqk,bhkd->bhqd', attn, v)
            out = out.transpose(0, 2, 1, 3).reshape(b, s, H * DH)
            out = out @ w_out.T + residual
            return (out, indices.astype(jnp.int64))
        return _reference_tuple_inner(x, w_down_q, w_down_kv, w_up_q, w_up_k, w_up_v, w_out, ln_scale, ln_bias)[0]

    def _L0_ffn_ref(x, centroids, ln_g, ln_b, w1, b1, w2, b2):
        import jax, jax.numpy as jnp
        import numpy as np
        LN_EPS = 1e-05

        def layer_norm(x, g, b):
            mu = jnp.mean(x, axis=-1, keepdims=True)
            var = jnp.var(x, axis=-1, keepdims=True)
            return (x - mu) / jnp.sqrt(var + LN_EPS) * g + b

        def balanced_assignment(scores):
            T, E = scores.shape
            C = T // E
            taken = jnp.zeros((T,), dtype=bool)
            parts = []
            for e in range(E):
                s = jnp.where(taken, -jnp.inf, scores[:, e])
                _, idx = jax.lax.top_k(s, C)
                parts.append(idx)
                taken = taken.at[idx].set(True)
            return jnp.concatenate(parts)
        D = x.shape[-1]
        feat = x.reshape(-1, D)
        T = feat.shape[0]
        E = centroids.shape[0]
        C = T // E
        norm = layer_norm(feat, ln_g, ln_b)
        scores = jax.lax.stop_gradient(norm @ centroids.T)
        sort_by_expert = balanced_assignment(scores)
        routed = feat[sort_by_expert].reshape(E, C, D)
        h = layer_norm(routed, ln_g, ln_b)
        h = jax.nn.gelu(jnp.einsum('ecd,edf->ecf', h, w1) + b1[:, None, :])
        h = jnp.einsum('ecf,efd->ecd', h, w2) + b2[:, None, :]
        out = routed + h
        inv = jnp.zeros((T,), dtype=jnp.int32).at[sort_by_expert].set(jnp.arange(T, dtype=jnp.int32))
        return out.reshape(T, D)[inv].reshape(x.shape)
    x = L0_attn_x
    xn = _layernorm(x, axis=-1)
    x = x + _L0_attn_ref(xn, L0_attn_w_down_q, L0_attn_w_down_kv, L0_attn_w_up_q, L0_attn_w_up_k, L0_attn_w_up_v, L0_attn_w_out, L0_attn_ln_scale, L0_attn_ln_bias) + _L0_ffn_ref(xn, L0_ffn_centroids, L0_ffn_ln_g, L0_ffn_ln_b, L0_ffn_w1, L0_ffn_b1, L0_ffn_w2, L0_ffn_b2)
    return x

_drawn_inputs = setup_inputs


def setup_inputs(seed=0):
    import zlib

    import numpy as np

    out = dict(_drawn_inputs(seed))
    spreads = {'L0_attn_ln_scale': (1.0, 0.6),
     'L0_attn_ln_bias': (0.0, 0.8),
     'L0_ffn_ln_g': (1.0, 0.6),
     'L0_ffn_ln_b': (0.0, 2.0),
     'L0_ffn_b1': (0.0, 2.0),
     'L0_ffn_b2': (0.0, 2.0)}
    factors = {'L0_attn_w_down_q': 8.0,
     'L0_attn_w_down_kv': 8.0,
     'L0_attn_w_up_q': 8.0,
     'L0_attn_w_up_k': 8.0,
     'L0_attn_w_up_v': 8.0,
     'L0_attn_w_out': 8.0,
     'L0_ffn_centroids': 6.77,
     'L0_ffn_w1': 8.0,
     'L0_ffn_w2': 6.857}
    for name, (base, spread) in spreads.items():
        noise = np.random.default_rng([zlib.crc32(name.encode()), seed]).standard_normal(out[name].shape)
        drawn = base * np.exp(spread * noise) if base else spread * noise
        out[name] = jnp.asarray(drawn.astype(out[name].dtype))
    for name, factor in factors.items():
        out[name] = (out[name] * factor).astype(out[name].dtype)
    return out
```

```python
from contextlib import ExitStack

import numpy as np

import concourse.bass as bass
from concourse import mybir

F32 = mybir.dt.float32
F32R = mybir.dt.float32r
I32 = mybir.dt.int32
ACT = mybir.ActivationFunctionType
ALU = mybir.AluOpType
AX = mybir.AxisListType
RADD = bass.bass_isa.ReduceOp.add

P = 128
S = 512
D = 256
KD = D // P
H = 16
DH = 64
L = 128
PAIRS = H // 2
TQ = S // P
E = 8
FF = 1024
NF = FF // P
EPS = 1e-5
SCALE = 1.0 / 8.0
BIG = -3.0e38
SHIFTS = [28, 25, 22, 19, 16, 13, 10, 7, 4, 1, 0]
CANDS = 7
MROWS = 2 * TQ


def layer_norm_stage(nc, t, B):
    sem = {}
    with ExitStack() as c:
        def sb(name, shape, dt=F32):
            return c.enter_context(nc.sbuf_tensor(name, shape, dt))

        for n in (*(f"{w}{k}" for w in ("x_loaded", "stored") for k in range(4)), "stats_ready", "aggr_ready", "rows_ready", "z_ready", "base_ready",
                  "zt_full", "norm_ready", "score_full", "score_copied", "tile_full", "tile_copied", "pool_step", "passed"):
            sem[n] = c.enter_context(nc.semaphore("ln_" + n))
        GB = min(4, B)
        x = sb("ln_x", [P, GB, TQ, D])
        st = sb("ln_stats", [P, GB, TQ, 6])
        mv = sb("ln_mv", [P, GB, TQ, 2])
        tmp = sb("ln_tmp", [P, 8, GB, TQ])
        rows = sb("ln_rows", [P, 3, GB, TQ])
        zb = sb("ln_zb", [P, GB, TQ, 2 * D])
        normT = sb("ln_normT", [P, 2, KD, S])
        scoreT = sb("ln_scoreT", [E, 2, S])
        ps_z = c.enter_context(nc.psum_tensor("ln_ps_z", [P, 2, KD, S], F32))
        ps_s = c.enter_context(nc.psum_tensor("ln_ps_s", [E, 2, S], F32))
        ps_t = c.enter_context(nc.psum_tensor("ln_ps_t", [P, 2, S], F32))
        block = c.enter_context(nc.Block())
        ROWS0, SLOT0 = GB, 2

        @block.sync
        def _(sp):
            with sp.Fori(0, B // GB) as i:
                for k in range(GB):
                    sp.wait_ge(sem["base_ready"], GB * i + k + 1)
                    sp.wait_ge(sem["z_ready"], GB * i + k + 1)
                    sp.dma_start(x[:, k], t["x"][GB * i + k].rearrange("(t p) d -> p t d", p=P)).then_inc(sem[f"x_loaded{k}"], 16)
                for k in range(GB):
                    sp.wait_ge(sem["z_ready"], GB * i + k + 1 + ROWS0)
                    sp.wait_ge(sem["base_ready"], GB * i + k + 1 + ROWS0)
                    sp.dma_start(t["rows_by_seq"][GB * i + k], zb[:, k]).then_inc(sem[f"stored{k}"], 16)
            for k in range(GB):
                sp.wait_ge(sem[f"stored{k}"], 16 * (B // GB) + 16)

        @block.vector
        def _(dve):
            with dve.Fori(0, B // GB) as i:
                for k in range(GB):
                    dve.wait_ge(sem[f"x_loaded{k}"], 16 * i + 16)
                    for q in range(TQ):
                        last = nc.vector.bn_stats(st[:, k, q], x[:, k, q])
                last.then_inc(sem["stats_ready"], 1)
                dve.wait_ge(sem["stats_ready"], i + 1)
                dve.sem_inc(sem["passed"], 1)
                for k in range(GB):
                    for q in range(TQ):
                        last = nc.vector.bn_aggr(mv[:, k, q], st[:, k, q])
                last.then_inc(sem["aggr_ready"], 1)
                dve.wait_ge(sem["rows_ready"], i + 1)
                for k in range(GB):
                    dve.wait_ge(sem[f"stored{k}"], 16 * i + 16)
                    for q in range(TQ):
                        last = nc.vector.tensor_scalar(zb[:, k, q, 0:D], x[:, k, q], mv[:, k, q, 0:1],
                                                       rows[:, 0, k, q:q + 1], ALU.subtract, ALU.mult)
                    last.then_inc(sem["z_ready"], 1)
                for k in range(GB + 1):
                    if k < GB:
                        dve.wait_ge(sem["score_full"], GB * i + k + 1 + SLOT0)
                        nc.vector.tensor_copy(scoreT[:, k % 2], ps_s[:, k % 2]).then_inc(sem["score_copied"], 1)
                    if k:
                        j = k - 1
                        dve.wait_ge(sem["tile_full"], GB * i + j + 1)
                        nc.vector.tensor_copy(
                            t["scores"][:, :, bass.ds((GB * i + j) * TQ, TQ)],
                            ps_t[:, j % 2, 0:TQ * E].rearrange("p (t e) -> p e t", e=E)).then_inc(sem["tile_copied"], 1)

        @block.gpsimd
        def _(pool):
            nc.gpsimd.memset(tmp[:, 7], -0.5).then_inc(sem["pool_step"], 1)
            pool.sem_inc(sem["base_ready"], ROWS0)
            pool.sem_inc(sem["z_ready"], ROWS0)
            for k in range(GB):
                pool.sem_inc(sem[f"stored{k}"], 16)
            with pool.Fori(0, B // GB) as i:
                pool.wait_ge(sem["aggr_ready"], i + 1)
                mean = mv[:, :, :, 0]
                var = mv[:, :, :, 1]
                steps = [
                    lambda: nc.gpsimd.tensor_scalar(tmp[:, 0], var, EPS, None, ALU.add),
                    lambda: nc.gpsimd.tensor_tensor(tmp[:, 1], tmp[:, 0], tmp[:, 7], ALU.pow),
                    lambda: nc.gpsimd.tensor_tensor(tmp[:, 2], var, tmp[:, 1], ALU.mult),
                    lambda: nc.gpsimd.tensor_tensor(tmp[:, 3], tmp[:, 2], tmp[:, 1], ALU.mult),
                    lambda: nc.gpsimd.tensor_scalar(tmp[:, 4], tmp[:, 3], EPS, None, ALU.add),
                    lambda: nc.gpsimd.tensor_tensor(tmp[:, 5], tmp[:, 4], tmp[:, 7], ALU.pow),
                    lambda: nc.gpsimd.tensor_tensor(rows[:, 0], tmp[:, 5], tmp[:, 1], ALU.mult),
                    lambda: nc.gpsimd.tensor_scalar(rows[:, 1], tmp[:, 1], 2.0, 1.0, ALU.mult, ALU.add),
                    lambda: nc.gpsimd.tensor_tensor(tmp[:, 6], mean, tmp[:, 1], ALU.mult),
                ]
                for j, step in enumerate(steps):
                    pool.wait_ge(sem["pool_step"], 9 * i + j + 1)
                    pool.sem_inc(sem["passed"], 1)
                    step().then_inc(sem["pool_step"], 1)
                pool.wait_ge(sem["pool_step"], 9 * i + 10)
                pool.sem_inc(sem["passed"], 1)
                nc.gpsimd.tensor_scalar(rows[:, 2], tmp[:, 6], -2.0, None, ALU.mult).then_inc(sem["rows_ready"], 1)

        @block.scalar
        def _(act):
            with act.Fori(0, B // GB) as i:
                act.wait_ge(sem["rows_ready"], i + 1)
                for j in range(GB + 1):
                    if j < GB:
                        act.wait_ge(sem[f"stored{j}"], 16 * i + 16)
                        for q in range(TQ):
                            last = nc.scalar.activation(zb[:, j, q, D:2 * D], x[:, j, q], ACT.Identity,
                                                        bias=rows[:, 2, j, q:q + 1], scale=rows[:, 1, j, q:q + 1])
                        last.then_inc(sem["base_ready"], 1)
                    if j:
                        k = j - 1
                        act.wait_ge(sem["zt_full"], GB * i + k + 1)
                        act.wait_ge(sem["score_full"], GB * i + k + 1)
                        for kd in range(KD):
                            last = nc.scalar.activation(normT[:, k % 2, kd], ps_z[:, k % 2, kd], ACT.Identity,
                                                        bias=t["ffn_b"][:, kd:kd + 1], scale=t["ffn_g"][:, kd:kd + 1])
                        last.then_inc(sem["norm_ready"], 1)

        @block.tensor
        def _(pe):
            for name in ("norm_ready", "score_copied", "tile_copied", "score_full"):
                pe.sem_inc(sem[name], SLOT0)
            with pe.Fori(0, B // GB) as i:
                for j in range(GB + 2):
                    if j < GB:
                        n = GB * i + j
                        pe.wait_ge(sem["z_ready"], n + 1 + ROWS0)
                        pe.wait_ge(sem["norm_ready"], n + 1)
                        for kd in range(KD):
                            for q in range(TQ):
                                last = nc.tensor.transpose(ps_z[:, j % 2, kd, q * P:(q + 1) * P],
                                                           zb[:, j, q, kd * P:(kd + 1) * P], t["ident"][:])
                        last.then_inc(sem["zt_full"], 1)
                    if 0 <= j - 1 < GB:
                        k = j - 1
                        n = GB * i + k
                        pe.wait_ge(sem["norm_ready"], n + 1 + SLOT0)
                        pe.wait_ge(sem["score_copied"], n + 1)
                        for kd in range(KD):
                            last = nc.tensor.matmul(ps_s[:, k % 2], t["centT"][:, kd], normT[:, k % 2, kd],
                                                    start=(kd == 0), stop=(kd == KD - 1))
                        last.then_inc(sem["score_full"], 1)
                    if 0 <= j - 2 < GB:
                        k = j - 2
                        n = GB * i + k
                        pe.wait_ge(sem["score_copied"], n + 1 + SLOT0)
                        pe.wait_ge(sem["tile_copied"], n + 1)
                        pe.sem_inc(sem["passed"], 1)
                        for q in range(TQ):
                            last = nc.tensor.transpose(ps_t[:, k % 2, q * E:(q + 1) * E],
                                                       scoreT[:, k % 2, q * P:(q + 1) * P], t["ident"][0:E, 0:E])
                        last.then_inc(sem["tile_full"], 1)


def routing_stage(nc, t, B):
    T = B * S
    C = T // E
    NT = T // P
    with ExitStack() as c:
        def sb(name, shape, dt=F32):
            return c.enter_context(nc.sbuf_tensor(name, shape, dt))

        def sem(name):
            return c.enter_context(nc.semaphore("rt_" + name))

        dve_step, asked, pool_sum, dve_sum, pe_sum, scattered, listed, idx_ready = [
            sem(n) for n in ("dve_step", "asked", "pool_sum", "dve_sum", "pe_sum", "scattered", "listed", "idx_ready")]
        v = sb("rt_v", [P, NT])
        avail = sb("rt_avail", [P, NT])
        pen = sb("rt_pen", [P, NT])
        w = sb("rt_work", [P, 12, NT])
        ge = sb("rt_ge", [P, CANDS, NT])
        cand = sb("rt_cand", [P, CANDS], I32)
        cur = sb("rt_cur", [P, 2], I32)
        step = sb("rt_step", [P, 1], I32)
        cnt = sb("rt_cnt", [P, CANDS])
        tot = sb("rt_tot", [P, CANDS])
        flags = sb("rt_flags", [P, CANDS])
        one = sb("rt_one", [P, 12])
        nrem = sb("rt_nrem", [P, 2])
        pos = sb("rt_pos", [P, NT])
        posi = sb("rt_posi", [P, NT], I32)
        ps = c.enter_context(nc.psum_tensor("rt_ps", [P, 2, S], F32))
        block = c.enter_context(nc.Block())

        ROUNDS = len(SHIFTS)
        POOL_SUMS = 1 + ROUNDS + 1
        PE_SUMS = 2

        @block.gpsimd
        def _(pool):
            with pool.Fori(0, E) as e:
                for j in range(POOL_SUMS):
                    k = CANDS if 1 <= j <= ROUNDS else 1
                    pool.wait_ge(dve_sum, POOL_SUMS * e + j + 1)
                    pool.sem_inc(asked, 1)
                    nc.gpsimd.partition_all_reduce(tot[:, 0:k], cnt[:, 0:k], P, RADD).then_inc(pool_sum, 1)
            pool.wait_ge(idx_ready, 1)
            for j in range(NT):
                pool.indirect_dma_start(
                    t["order"], bass.IndirectOffsetOnAxis(ap=posi[:, j:j + 1], axis=0),
                    t["token_ids"][:, j:j + 1], None).then_inc(scattered, 16)
            pool.wait_ge(scattered, 16 * NT)

        @block.tensor
        def _(pe):
            with pe.Fori(0, E) as e:
                for j in range(PE_SUMS):
                    src = w[:, 10 + j]
                    pe.wait_ge(listed, PE_SUMS * e + j + 1)
                    nc.tensor.matmul(ps[:, 0, 0:NT], t["before"][:], src, start=True, stop=True)
                    nc.tensor.matmul(ps[:, 1, 0:NT], t["ones"][:], src, start=True, stop=True).then_inc(pe_sum, 1)

        @block.vector
        def _(dve):
            count = [0]
            base = [0]

            def link(ins, to=None, loop=None):
                ins.then_inc(dve_step, 1)
                count[0] += 1
                dve.wait_ge(dve_step, base[0] + count[0])
                return ins

            V = nc.vector
            link(V.memset(avail[:], 1.0))
            link(V.memset(pen[:], 0.0))
            link(V.memset(pos[:], 0.0))
            link(V.memset(nrem[:, 0:1], float(T)))
            link(V.memset(nrem[:, 1:2], 0.0))
            start = count[0]
            body_steps = [None]

            def body(e, per):
                count[0] = 0
                base[0] = start + per * e
                sums = [0]
                lists = [0]

                def summed(k):
                    sums[0] += 1
                    dve.sem_inc(dve_sum, 1)
                    dve.wait_ge(pool_sum, POOL_SUMS * e + sums[0])

                def prefix(dst, srcslot, tmp):
                    lists[0] += 1
                    dve.sem_inc(listed, 1)
                    dve.wait_ge(pe_sum, PE_SUMS * e + lists[0])
                    link(V.tensor_copy(w[:, tmp], ps[:, 1, 0:NT]))
                    link(V.tensor_tensor_scan(w[:, tmp + 1], w[:, tmp], w[:, tmp], 0.0, ALU.add, ALU.bypass))
                    link(V.tensor_tensor(w[:, tmp + 1], w[:, tmp + 1], w[:, tmp], ALU.subtract))
                    link(V.tensor_tensor(dst, ps[:, 0, 0:NT], w[:, tmp + 1], ALU.add))

                s = t["scores"][:, e, :] if isinstance(e, int) else t["scores"][:, bass.ds(e, 1), :].rearrange("p o t -> p (o t)")
                neg, K, thr = one[:, 0:1], one[:, 1:2], cur[:, 0:1]
                link(V.tensor_tensor(v[:], s, avail[:], ALU.mult))
                link(V.tensor_tensor(v[:], v[:], pen[:], ALU.add))
                link(V.tensor_scalar(w[:, 0], v[:], 0.0, None, ALU.is_ge, ALU.add, accum_out=cnt[:, 0:1]))
                summed(1)
                link(V.tensor_scalar(neg, tot[:, 0:1], float(C), None, ALU.is_lt))
                link(V.tensor_scalar(one[:, 2:3], neg, -2.0, 1.0, ALU.mult, ALU.add))
                link(V.tensor_scalar(one[:, 3:4], nrem[:, 0:1], 1.0 - 2.0 * C, None, ALU.add))
                link(V.tensor_tensor(one[:, 4:5], one[:, 3:4], neg, ALU.mult))
                link(V.tensor_scalar(K, one[:, 4:5], float(C), None, ALU.add))
                link(V.tensor_scalar(w[:, 0], s, one[:, 2:3], None, ALU.mult))
                link(V.tensor_tensor(w[:, 1], w[:, 0], avail[:], ALU.mult))
                link(V.tensor_tensor(v[:], w[:, 1], pen[:], ALU.add))
                link(V.memset(cur[:], 0))
                for r, shift in enumerate(SHIFTS):
                    link(V.tensor_tensor(cand[:], t["cand_bits"][:, r], cur[:, 0:1].broadcast_to([P, CANDS]), ALU.bitwise_or))
                    link(V.tensor_tensor(ge[:], v[:].unsqueeze(1).broadcast_to([P, CANDS, NT]),
                                         cand[:].bitcast(F32).unsqueeze(2).broadcast_to([P, CANDS, NT]), ALU.is_ge))
                    link(V.tensor_reduce(cnt[:], ge[:], AX.X, ALU.add))
                    summed(CANDS)
                    width = 1 if r == ROUNDS - 1 else CANDS
                    link(V.tensor_scalar(flags[:, 0:width], tot[:, 0:width], K, None, ALU.is_ge, ALU.add, accum_out=one[:, 5:6]))
                    link(V.tensor_scalar(step[:], one[:, 5:6], float(1 << shift), None, ALU.mult))
                    link(V.tensor_tensor(cur[:, 0:1], cur[:, 0:1], step[:], ALU.bitwise_or))
                thrf = thr.bitcast(F32)
                link(V.tensor_scalar(w[:, 10], v[:], thrf, None, ALU.is_equal))
                link(V.tensor_scalar(w[:, 1], v[:], thrf, None, ALU.is_ge))
                link(V.tensor_tensor(w[:, 2], w[:, 1], w[:, 10], ALU.subtract))
                link(V.tensor_tensor(w[:, 3], avail[:], w[:, 1], ALU.subtract))
                link(V.tensor_tensor(w[:, 3], w[:, 3], w[:, 2], ALU.subtract))
                link(V.tensor_scalar(w[:, 3], w[:, 3], neg, None, ALU.mult))
                link(V.tensor_tensor(w[:, 4], w[:, 3], w[:, 2], ALU.add))
                link(V.reduce_sum(cnt[:, 0:1], w[:, 4], AX.X))
                summed(1)
                link(V.tensor_scalar(one[:, 6:7], tot[:, 0:1], -1.0, float(C), ALU.mult, ALU.add))
                prefix(w[:, 5], 10, 6)
                link(V.tensor_scalar(w[:, 5], w[:, 5], one[:, 6:7], None, ALU.is_lt))
                link(V.tensor_tensor(w[:, 5], w[:, 5], w[:, 10], ALU.mult))
                link(V.tensor_tensor(w[:, 11], w[:, 5], w[:, 4], ALU.add))
                prefix(w[:, 5], 11, 6)
                link(V.tensor_scalar(w[:, 5], w[:, 5], nrem[:, 1:2], None, ALU.add))
                link(V.tensor_tensor(w[:, 5], w[:, 5], w[:, 11], ALU.mult))
                link(V.tensor_tensor(pos[:], pos[:], w[:, 5], ALU.add))
                link(V.tensor_tensor(avail[:], avail[:], w[:, 11], ALU.subtract))
                link(V.tensor_scalar(pen[:], avail[:], -BIG, BIG, ALU.mult, ALU.add))
                link(V.tensor_scalar(nrem[:, 0:1], nrem[:, 0:1], -float(C), None, ALU.add))
                link(V.tensor_scalar(nrem[:, 1:2], nrem[:, 1:2], float(C), None, ALU.add))
                return count[0]

            STEPS = 12 + 6 * ROUNDS + 8 + 1 + 4 + 3 + 4 + 7
            with dve.Fori(0, E) as e:
                n = body(e, STEPS)
            assert n == STEPS, (n, STEPS)
            V.tensor_copy(posi[:], pos[:]).then_inc(idx_ready, 1)


def attention_stage(nc, t, a, B):
    R = F32R
    with ExitStack() as c:
        def sb(name, shape, dt=F32):
            return c.enter_context(nc.sbuf_tensor("at_" + name, shape, dt))

        def sem(name):
            return c.enter_context(nc.semaphore("at_" + name))

        wq = sb("wq", [P, 2, 2, H * DH], R)
        wk = sb("wk", [P, 2, 2, H * DH], R)
        wv = sb("wv", [P, 2, H * DH], R)
        wd = sb("wd", [P, 2, KD, 2, L], R)
        wo = sb("wo", [P, PAIRS, D])
        cos = sb("cos", [P, S])
        sin = sb("sin", [P, S])
        own = sb("own", [MROWS, MROWS])
        gb = sb("gb", [P, 2, KD])

        with ExitStack() as w:
            raw = {n: w.enter_context(nc.sbuf_tensor("at_raw_" + n, s, F32)) for n, s in
                   (("wq", [P, 2, H * DH]), ("wk", [P, 2, H * DH]), ("wv", [P, H * DH]), ("wd", [P, KD, 2, L]))}
            got = w.enter_context(nc.semaphore("at_weights_loaded"))
            rounded = w.enter_context(nc.semaphore("at_weights_rounded"))
            split = w.enter_context(nc.semaphore("at_weights_split"))
            block = w.enter_context(nc.Block())
            loads = [
                (raw["wq"][:], a["wq"]), (raw["wk"][:], a["wk"]), (raw["wv"][:], a["wv"]),
                (raw["wd"][:, :, 0], a["wdqT"].rearrange("(k p) l -> p k l", p=P)),
                (raw["wd"][:, :, 1], a["wdkvT"].rearrange("(k p) l -> p k l", p=P)),
                (wo[:], a["woT"].rearrange("(h p) d -> p h d", p=P)),
                (cos[:], a["cos"]), (sin[:], a["sin"]), (own[:], a["own_tile"]),
                (gb[:, 0], a["attn_g"]), (gb[:, 1], a["attn_b"]),
            ]

            @block.sync
            def _(sp):
                for dst, src in loads:
                    sp.dma_start(dst, src).then_inc(got, 16)
                sp.wait_ge(got, 16 * len(loads))

            @block.vector
            def _(dve):
                dve.wait_ge(got, 16 * len(loads))
                for n, (name, dst) in enumerate((("wq", wq), ("wk", wk), ("wv", wv), ("wd", wd))):
                    nc.vector.tensor_copy(dst[:, 0], raw[name][:]).then_inc(rounded, 1)
                    dve.wait_ge(rounded, n + 1)
                    nc.vector.tensor_tensor(dst[:, 1], raw[name][:], dst[:, 0].bitcast(F32), ALU.subtract).then_inc(split, 1)

        z = sb("z", [P, TQ, D])
        res = sb("res", [P, TQ, D])
        h32 = sb("h32", [P, 2, S])
        hs = sb("hs", [P, 2, KD, S], R)
        cl = sb("cl", [P, 2, 2, S], R)
        V = sb("V", [P, TQ, H * DH])
        rot = sb("rot", [P, 4, S])
        qr = sb("qr", [P, S])
        kr = sb("kr", [P, S])
        kA = sb("kA", [P, 2, 2, S], R)
        kB = sb("kB", [P, 2, 2, S], R)
        qC = sb("qC", [P, 2, 2, S], R)
        qD = sb("qD", [P, 2, 2, S], R)
        mx = sb("mx", [P, MROWS])
        probs = sb("probs", [P, 2, TQ, 2, S])
        psum_k = sb("psum_k", [P, 2, S])
        den_t = sb("den_t", [P, S])
        rec_col = sb("rec_col", [P, S // 32])
        rec = sb("rec", [P, S])
        oT = sb("oT", [P, PAIRS, S])
        ring = [c.enter_context(nc.psum_tensor(f"at_ring{i}", [P, 2, S], F32)) for i in range(2)]
        mb = c.enter_context(nc.psum_tensor("at_maxima", [P, 2, S], F32))
        po = c.enter_context(nc.psum_tensor("at_out", [P, S], F32))
        xb = c.enter_context(nc.psum_tensor("at_mixed", [P, S], F32))

        ring_full, ring_read = sem("ring_full"), sem("ring_read")
        x_full, x_read = sem("x_full"), sem("x_read")
        m_full, m_read = sem("m_full"), sem("m_read")
        mt_full, m_rows = sem("mt_full"), sem("m_rows")
        pv_full, o_done = sem("pv_full"), sem("o_done")
        out_full, out_done = sem("out_full"), sem("out_done")
        qr_ready, kr_ready = sem("qr_ready"), sem("kr_ready")
        hi_ready, kb_ready = sem("hi_ready"), sem("kb_ready")
        alo_ready, qlo_ready = sem("alo_ready"), sem("qlo_ready")
        summed = sem("summed")
        rec_step = sem("rec_step")
        h32_ready, hhi_ready, hlo_ready = sem("h32_ready"), sem("hhi_ready"), sem("hlo_ready")
        c32_ready, chi_ready, clo_ready = sem("c32_ready"), sem("chi_ready"), sem("clo_ready")
        z_loaded, res_loaded, res_stored = sem("z_loaded"), sem("res_loaded"), sem("res_stored")
        start = sem("start")

        PV0, SUM0, O0, OUT0, STORED0 = 2, 6, 1, 1, 16
        PER_SEQ = TQ + PAIRS * TQ + 2

        def ring_local(b, kind, p=0, kt=0):
            last = isinstance(b, int) and b == B - 1
            if kind == "V":
                return kt
            if kind == "z":
                return TQ + 5 * TQ
            if kind == "c":
                return TQ + 6 * TQ + 1
            return TQ + TQ * p + kt + (0 if last else (p >= 5) + (p >= 6))

        def ring_at(b, kind, p=0, kt=0):
            return 2 + PER_SEQ * b + ring_local(b, kind, p, kt)

        def x_order(last):
            order = []
            for p in range(PAIRS):
                order += [("den", p - 1)] if p else []
                order += [(w, p + 2) for w in ("qA", "qB", "kA", "kB")] if p + 2 < PAIRS or not last else []
            return order + [("den", PAIRS - 1)]

        X = {last: {u: n for n, u in enumerate(x_order(last))} for last in (False, True)}
        X_PER_SEQ = len(X[False])

        def x_at(b, last, use):
            return 8 + X_PER_SEQ * b + X[last][use]

        WHAT = {"qA": (wq, 0, 0), "qB": (wq, 1, 0), "kA": (wk, 0, 1), "kB": (wk, 1, 1)}

        block = c.enter_context(nc.Block())

        @block.sync
        def _(sp):
            def load_z(b):
                sp.dma_start(z[:], t["rows_by_seq"][b][:, :, 0:D]).then_inc(z_loaded, 16)

            def body(b, last):
                if not last:
                    sp.wait_ge(ring_full, ring_at(b, "V") + 1)
                    load_z(b + 1)
                sp.wait_ge(res_stored, 16 * b + STORED0)
                sp.dma_start(res[:], t["rows_by_seq"][b][:, :, D:2 * D]).then_inc(res_loaded, 16)
                sp.wait_ge(out_done, b + 1 + OUT0)
                sp.dma_start(t["rows_by_seq"][b][:, :, D:2 * D], res[:]).then_inc(res_stored, 16)

            load_z(0)
            sp.sem_inc(res_stored, STORED0)
            with sp.Fori(0, B - 1) as b:
                body(b, False)
            body(B - 1, True)
            sp.wait_ge(res_stored, 16 * B + STORED0)

        @block.tensor
        def _(pe):
            T = nc.tensor

            def mm3(dst, w, x, first, last):
                T.matmul(dst, w[0], x[0], start=first, stop=False)
                T.matmul(dst, w[0], x[1], start=False, stop=False)
                return T.matmul(dst, w[1], x[0], start=False, stop=last)

            def ring_slot(n, local):
                if not (isinstance(n, int) and n < 2):
                    pe.wait_ge(ring_read, n - 1)
                return ring[local % 2]

            def transpose_z(b, n):
                pe.wait_ge(z_loaded, 16 * b + 16)
                slot = ring_slot(n, 0)
                for kd in range(KD):
                    for q in range(TQ):
                        last = T.transpose(slot[:, kd, q * P:(q + 1) * P], z[:, q, kd * P:(kd + 1) * P], t["ident"][:])
                last.then_inc(ring_full, 1)

            def latents(b, n):
                pe.wait_ge(hlo_ready, b + 1)
                pe.wait_ge(hhi_ready, b + 1)
                slot = ring_slot(n, 1)
                for w in range(2):
                    for kd in range(KD):
                        last = mm3(slot[:, w], [wd[:, i, kd, w] for i in range(2)], [hs[:, i, kd] for i in range(2)],
                                   kd == 0, kd == KD - 1)
                last.then_inc(ring_full, 1)

            def values(b):
                for kt in range(TQ):
                    slot = ring_slot(ring_at(b, "V", 0, kt), kt)
                    for n in range(2):
                        last = mm3(slot[:, n], [cl[:, i, 1, kt * P:(kt + 1) * P] for i in range(2)],
                                   [wv[:, i, n * S:(n + 1) * S] for i in range(2)], True, True)
                    last.then_inc(ring_full, 1)

            def project(n, what, p, seq):
                if n is not None:
                    pe.wait_ge(x_read, n)
                if p % PAIRS == 0 and what == "qA":
                    pe.wait_ge(clo_ready, seq + 1)
                    pe.wait_ge(chi_ready, seq + 1)
                w, swap, which = WHAT[what]
                cols = slice((p % PAIRS) * P, (p % PAIRS + 1) * P)
                mm3(xb[:], [w[:, i, swap, cols] for i in range(2)], [cl[:, i, which] for i in range(2)],
                    True, True).then_inc(x_full, 1)

            def maxima(g, p, j, b=None):
                par, head = p % 2, j // 2
                if not (isinstance(g, int) and g == 0 and j == 0):
                    pe.wait_ge(m_read, 4 * g + j)
                if j == 0 and p:
                    pe.wait_ge(m_rows, g)
                if j == 0 and p == 1:
                    pe.wait_ge(out_done, b + OUT0)
                if j % 2 == 0:
                    pe.wait_ge(alo_ready, 2 * g + head + 1)
                for i in range(2):
                    q = 2 * (j % 2) + i
                    last = T.matmul(mb[:, i], qC[:, par, head, q * P:(q + 1) * P], kA[:, par, head], start=True, stop=True)
                last.then_inc(m_full, 1)

            def maxima_rows(g):
                pe.wait_ge(m_read, 4 * g + 4)
                T.transpose(mb[0:MROWS, 0, 0:P], mx[:], t["ident"][:]).then_inc(mt_full, 1)

            def scores(b, g, p, kt):
                par = p % 2
                n = ring_at(b, "S", p, kt)
                slot = ring_slot(n, ring_local(b, "S", p, kt))
                if kt == 0:
                    pe.wait_ge(m_rows, g + 1)
                    pe.wait_ge(qlo_ready, 2 * g + 2)
                    pe.wait_ge(kb_ready, g + 1)
                keys = slice(kt * P, (kt + 1) * P)
                for head in range(2):
                    T.matmul(slot[:, head], kA[:, par, head, keys], qC[:, par, head], start=True, stop=False)
                    last = T.matmul(slot[:, head], kB[0:DH + MROWS, par, head, keys], qD[0:DH + MROWS, par, head],
                                    start=False, stop=True)
                last.then_inc(ring_full, 1)

            def times_v(b, g, p, kt):
                if kt == 0:
                    pe.wait_ge(o_done, g + O0)
                pe.wait_ge(ring_read, ring_at(b, "S", p, kt) + 1)
                for head in range(2):
                    h = 2 * p + head
                    last = T.matmul(po[head * DH:(head + 1) * DH], V[:, kt, h * DH:(h + 1) * DH],
                                    probs[:, p % 2, kt, head], start=(kt == 0), stop=(kt == TQ - 1))
                if kt == TQ - 1:
                    last.then_inc(pv_full, 1)

            def denominators(b, last_seq, g, p):
                pe.wait_ge(x_read, x_at(b, last_seq, ("den", p)))
                pe.wait_ge(summed, 3 * g + 3 + SUM0)
                for head in range(2):
                    last = T.matmul(xb[head * DH:(head + 1) * DH], t["ones"][:, 0:DH], psum_k[:, head], start=True, stop=True)
                last.then_inc(x_full, 1)

            def out_pair(b, p):
                pe.wait_ge(o_done, PAIRS * b + p + 1 + O0)
                for q in range(TQ):
                    last = T.matmul(mb[:, q // 2, (q % 2) * D:(q % 2 + 1) * D], oT[:, p, q * P:(q + 1) * P], wo[:, p],
                                    start=(p == 0 and q % 2 == 0), stop=(p == PAIRS - 1), skip_group_check=True)
                if p == PAIRS - 1:
                    last.then_inc(out_full, 1)

            def body(b, last):
                values(b)
                for p in range(PAIRS):
                    g = PAIRS * b + p
                    prev = (b, g - 1, p - 1)
                    ahead = not last or p + 2 < PAIRS
                    nxt = not last or p + 1 < PAIRS

                    def proj(what):
                        if ahead:
                            project(x_at(b, last, (what, p + 2)), what, p + 2, b + (p + 2) // PAIRS)

                    def mxs(j):
                        if nxt:
                            maxima(g + 1, p + 1, j, b)

                    if p:
                        times_v(*prev, 0)
                        times_v(*prev, 1)
                    scores(b, g, p, 0)
                    scores(b, g, p, 1)
                    if p:
                        denominators(b, last, g - 1, p - 1)
                    mxs(0)
                    proj("qA")
                    if p:
                        times_v(*prev, 2)
                    mxs(1)
                    proj("qB")
                    scores(b, g, p, 2)
                    if p:
                        times_v(*prev, 3)
                    mxs(2)
                    proj("kA")
                    mxs(3)
                    scores(b, g, p, 3)
                    proj("kB")
                    if nxt:
                        maxima_rows(g + 1)
                    if p == 4 and not last:
                        transpose_z(b + 1, ring_at(b, "z"))
                    if p == 5 and not last:
                        latents(b + 1, ring_at(b, "c"))
                g = PAIRS * b + PAIRS - 1
                pe.wait_ge(m_rows, g + 1 if last else g + 2)
                for p in range(PAIRS - 2):
                    out_pair(b, p)
                for kt in range(TQ):
                    times_v(b, g, PAIRS - 1, kt)
                denominators(b, last, g, PAIRS - 1)
                for p in (PAIRS - 2, PAIRS - 1):
                    out_pair(b, p)

            pe.wait_ge(start, 1)
            transpose_z(0, 0)
            latents(0, 1)
            for p in range(2):
                for j, what in enumerate(("qA", "qB", "kA", "kB")):
                    project(4 * p + j if p + j else None, what, p, 0)
            for j in range(4):
                maxima(0, 0, j)
            maxima_rows(0)
            with pe.Fori(0, B - 1) as b:
                body(b, False)
            body(B - 1, True)

        @block.scalar
        def _(act):
            A = nc.scalar

            def normed(b, n):
                act.wait_ge(ring_full, n + 1)
                if not (isinstance(b, int) and b == 0):
                    act.wait_ge(clo_ready, b)
                slot = ring[0]
                for kd in range(KD):
                    last = A.activation(h32[:, kd], slot[:, kd], ACT.Identity, bias=gb[:, 1, kd:kd + 1], scale=gb[:, 0, kd:kd + 1])
                    if kd == 0:
                        last.then_inc(h32_ready, 1)
                    else:
                        last.then_inc(ring_read, 1)
                act.wait_ge(ring_read, n + 1)
                act.wait_ge(h32_ready, b + 1)
                A.copy(hs[:, 0], h32[:]).then_inc(hhi_ready, 1)

            def latent(b, n, last_use):
                act.wait_ge(ring_full, n + 1)
                act.wait_ge(hlo_ready, b + 1)
                A.copy(h32[:], ring[1][:]).then_inc(ring_read, 1)
                act.wait_ge(ring_read, n + 1)
                if last_use is not None:
                    act.wait_ge(x_full, last_use)
                A.copy(cl[:, 0], h32[:]).then_inc(chi_ready, 1)

            def rounded(g, p, head, ring_done):
                par, s = p % 2, slice(head * DH, (head + 1) * DH)
                o = slice((1 - head) * DH, (2 - head) * DH)
                if head == 0:
                    act.wait_ge(qr_ready, g + 1)
                    if ring_done is not None:
                        act.wait_ge(ring_full, ring_done)
                A.copy(qC[s, par, head], qr[s])
                A.copy(qC[o, par, head], qr[s])
                if head == 0:
                    act.wait_ge(kr_ready, g + 1)
                A.copy(kA[s, par, head], kr[s]).then_inc(hi_ready, 1)

            def rounded_k(p):
                par = p % 2
                for head in range(2):
                    last = A.copy(kB[0:DH, par, head], kr[head * DH:(head + 1) * DH])
                last.then_inc(kb_ready, 1)

            def exps(b, g, p, kt):
                n = ring_at(b, "S", p, kt)
                act.wait_ge(ring_full, n + 1)
                if kt == 0:
                    act.wait_ge(pv_full, g - 1 + PV0)
                    act.wait_ge(summed, 3 * g - 3 + SUM0)
                A.activation(probs[:, p % 2, kt], ring[ring_local(b, "S", p, kt) % 2][:], ACT.Exp, scale=SCALE).then_inc(ring_read, 1)

            def body(b, last):
                for kt in range(TQ):
                    n = ring_at(b, "V", 0, kt)
                    act.wait_ge(ring_full, n + 1)
                    if kt == 0:
                        act.wait_ge(pv_full, PAIRS * b + PV0)
                    A.copy(V[:, kt].rearrange("p (n s) -> p n s", n=2), ring[kt % 2][:]).then_inc(ring_read, 1)
                for p in range(PAIRS):
                    g = PAIRS * b + p
                    nxt = not last or p + 1 < PAIRS
                    done = ring_at(b, "V") if p == 0 else ring_at(b, "S", p - 1, TQ - 1) + 1
                    if nxt:
                        rounded(g + 1, p + 1, 0, done)
                    exps(b, g, p, 0)
                    if nxt:
                        rounded(g + 1, p + 1, 1, None)
                    exps(b, g, p, 1)
                    if nxt:
                        rounded_k(p + 1)
                    exps(b, g, p, 2)
                    exps(b, g, p, 3)
                    if p == 4 and not last:
                        normed(b + 1, ring_at(b, "z"))
                    if p == 5 and not last:
                        latent(b + 1, ring_at(b, "c"), x_at(b, last, ("kB", PAIRS - 1)) + 1)

            act.wait_ge(start, 1)
            normed(0, 0)
            latent(0, 1, None)
            rounded(0, 0, 0, None)
            rounded(0, 0, 1, None)
            rounded_k(0)
            with act.Fori(0, B - 1) as b:
                body(b, False)
            body(B - 1, True)

        @block.vector
        def _(dve):
            V_ = nc.vector

            def k_rest(g, p, head):
                par, s = p % 2, slice(head * DH, (head + 1) * DH)
                o = slice((1 - head) * DH, (2 - head) * DH)
                dve.wait_ge(hi_ready, 2 * g + head + 1)
                V_.tensor_tensor(kA[o, par, head], kr[s], kA[s, par, head].bitcast(F32), ALU.subtract).then_inc(alo_ready, 1)

            def q_rest(g, p, head):
                par, s = p % 2, slice(head * DH, (head + 1) * DH)
                V_.tensor_tensor(qD[0:DH, par, head], qr[s], qC[s, par, head].bitcast(F32), ALU.subtract).then_inc(qlo_ready, 1)

            def reduce(g, j):
                dve.wait_ge(m_full, 4 * g + j + 1)
                V_.tensor_reduce(mx[:, 2 * j:2 * j + 2], mb[:], AX.X, ALU.max, negate=True).then_inc(m_read, 1)

            def rotate(n, what, g):
                dve.wait_ge(x_full, n + 1)
                q = what[0] == "q"
                if what[1] == "A" and not (isinstance(g, int) and g == 0):
                    dve.wait_ge(qr_ready if q else kr_ready, g)
                V_.tensor_tensor(rot[:, (0 if q else 2) + (what[1] == "B")], xb[:], (sin if what[1] == "B" else cos)[:],
                                 ALU.mult).then_inc(x_read, 1)

            def row_maxima(g, p):
                dve.wait_ge(mt_full, g + 1)
                par = p % 2
                V_.tensor_tensor(qD[DH:DH + MROWS, par].rearrange("r h (t n) -> r (h t) n", t=TQ),
                                 mb[0:MROWS, 0, 0:P].unsqueeze(1).broadcast_to([MROWS, MROWS, P]),
                                 own[:].unsqueeze(2).broadcast_to([MROWS, MROWS, P]), ALU.mult).then_inc(m_rows, 1)

            def den_rows(b, last, g, p):
                dve.wait_ge(x_full, x_at(b, last, ("den", p)) + 1)
                V_.transpose(den_t[:], xb[:]).then_inc(x_read, 1)

            def reciprocals(b, last, g, p):
                dve.wait_ge(x_read, x_at(b, last, ("den", p)) + 1)
                V_.reciprocal(rec_col[:], den_t[:, ::32]).then_inc(rec_step, 1)
                dve.wait_ge(rec_step, 2 * g + 1)
                V_.transpose(rec[:], rec_col[:].unsqueeze(2).broadcast_to([P, S // 32, 32])).then_inc(rec_step, 1)

            def normalise(b, last, g, p):
                dve.wait_ge(rec_step, 2 * g + 2)
                dve.wait_ge(pv_full, g + 1 + PV0)
                if p == 0:
                    dve.wait_ge(out_full, b + OUT0)
                V_.tensor_tensor(oT[:, p], po[:], rec[:], ALU.mult).then_inc(o_done, 1)

            def body(b, last):
                for p in range(PAIRS):
                    g = PAIRS * b + p
                    ahead = not last or p + 2 < PAIRS
                    nxt = not last or p + 1 < PAIRS

                    def turn(what):
                        if ahead:
                            rotate(x_at(b, last, (what, p + 2)), what, g + 2)

                    def red(j):
                        if nxt:
                            reduce(g + 1, j)

                    if nxt:
                        k_rest(g + 1, p + 1, 0)
                        q_rest(g + 1, p + 1, 0)
                    if p:
                        den_rows(b, last, g - 1, p - 1)
                    red(0)
                    if nxt:
                        k_rest(g + 1, p + 1, 1)
                    turn("qA")
                    if p:
                        reciprocals(b, last, g - 1, p - 1)
                    red(1)
                    turn("qB")
                    if nxt:
                        q_rest(g + 1, p + 1, 1)
                    red(2)
                    turn("kA")
                    if p:
                        normalise(b, last, g - 1, p - 1)
                    red(3)
                    turn("kB")
                    if nxt:
                        row_maxima(g + 1, p + 1)
                g = PAIRS * b + PAIRS - 1
                den_rows(b, last, g, PAIRS - 1)
                reciprocals(b, last, g, PAIRS - 1)
                normalise(b, last, g, PAIRS - 1)
                dve.wait_ge(out_full, b + 1 + OUT0)
                dve.wait_ge(res_loaded, 16 * b + 16)
                V_.tensor_tensor(res[:].rearrange("p (i q) d -> p i (q d)", i=2), res[:].rearrange("p (i q) d -> p i (q d)", i=2),
                                 mb[:], ALU.add).then_inc(out_done, 1)

            for par in range(2):
                last = V_.memset(kB[DH:DH + MROWS, par].bitcast(F32), 1.0)
            last.then_inc(start, 1)
            dve.sem_inc(out_done, OUT0)
            dve.sem_inc(out_full, OUT0)
            dve.sem_inc(o_done, O0)
            dve.sem_inc(pv_full, PV0)
            dve.sem_inc(summed, SUM0)
            for p in range(2):
                for j, what in enumerate(("qA", "qB", "kA", "kB")):
                    rotate(4 * p + j, what, p)
                if p == 0:
                    for head in range(2):
                        k_rest(0, 0, head)
                        q_rest(0, 0, head)
            for j in range(4):
                reduce(0, j)
            row_maxima(0, 0)
            with dve.Fori(0, B - 1) as b:
                body(b, False)
            body(B - 1, True)

        @block.gpsimd
        def _(pool):
            G = nc.gpsimd

            def rest(dst, src, hi, ready, n, done):
                pool.wait_ge(ready, n)
                G.tensor_tensor(dst, src, hi.bitcast(F32), ALU.subtract).then_inc(done, 1)

            def sum_q(n, g):
                pool.wait_ge(x_read, n + 1)
                if not (isinstance(g, int) and g == 0):
                    pool.wait_ge(hi_ready, 2 * g)
                    pool.wait_ge(qlo_ready, 2 * g)
                G.tensor_tensor(qr[:], rot[:, 0], rot[:, 1], ALU.add).then_inc(qr_ready, 1)

            def sum_k(n, g):
                pool.wait_ge(x_read, n + 1)
                if not (isinstance(g, int) and g == 0):
                    pool.wait_ge(alo_ready, 2 * g)
                    pool.wait_ge(kb_ready, g)
                G.tensor_tensor(kr[:], rot[:, 2], rot[:, 3], ALU.add).then_inc(kr_ready, 1)

            def add(b, g, p, kt, free=None):
                pool.wait_ge(ring_read, ring_at(b, "S", p, kt) + 1)
                if kt == 1:
                    pool.wait_ge(x_full, free)
                    src = probs[:, p % 2, 0]
                else:
                    pool.wait_ge(summed, 3 * g + kt - 1 + SUM0)
                    src = psum_k[:]
                G.tensor_tensor(psum_k[:], src, probs[:, p % 2, kt], ALU.add).then_inc(summed, 1)

            def body(b, last):
                for p in range(PAIRS):
                    g = PAIRS * b + p
                    ahead = not last or p + 2 < PAIRS
                    free = 8 + X_PER_SEQ * b if p == 0 else x_at(b, last, ("den", p - 1)) + 1
                    add(b, g, p, 1, free)
                    if ahead:
                        sum_q(x_at(b, last, ("qB", p + 2)), g + 2)
                    add(b, g, p, 2)
                    if ahead:
                        sum_k(x_at(b, last, ("kB", p + 2)), g + 2)
                    add(b, g, p, 3)
                    if p == 4 and not last:
                        rest(hs[:, 1], h32[:], hs[:, 0], hhi_ready, b + 2, hlo_ready)
                    if p == 5 and not last:
                        rest(cl[:, 1], h32[:], cl[:, 0], chi_ready, b + 2, clo_ready)

            pool.wait_ge(start, 1)
            rest(hs[:, 1], h32[:], hs[:, 0], hhi_ready, 1, hlo_ready)
            rest(cl[:, 1], h32[:], cl[:, 0], chi_ready, 1, clo_ready)
            for p in range(2):
                sum_q(4 * p + 1, p)
                sum_k(4 * p + 3, p)
            with pool.Fori(0, B - 1) as b:
                body(b, False)
            body(B - 1, True)


def ffn_stage(nc, t, a, B):
    R = F32R
    C = B * S // E
    UT = min(S, C)
    TU = UT // P
    UNITS = C // UT
    CT = C // P
    NB = 2 * UNITS
    AHEAD = NB // 2
    out_rows = t["out"].rearrange("b s d -> (b s) d")
    with ExitStack() as c:
        def sb(name, shape, dt=F32):
            return c.enter_context(nc.sbuf_tensor("ff_" + name, shape, dt))

        def sem(name):
            return c.enter_context(nc.semaphore("ff_" + name))

        raw1 = sb("raw1", [P, KD, FF])
        raw2 = sb("raw2", [P, NF, D])
        w1 = [sb(f"w1_{k}", [P, 2, KD, FF], R) for k in range(2)]
        w2 = [sb(f"w2_{k}", [P, 2, NF, D], R) for k in range(2)]
        idx = [sb(f"idx{k}", [P, CT], I32) for k in range(2)]
        primer = sb("primer", [P, NB], I32)
        b1 = [sb(f"b1_{k}", [P, NF]) for k in range(2)]
        b2 = [sb(f"b2_{k}", [P, D]) for k in range(2)]
        rows = [sb(f"rows{u}", [P, TU, 2 * D]) for u in range(NB)]
        n32 = sb("n32", [P, KD, UT])
        nT = [sb(f"nT{k}", [P, 2, KD, UT], R) for k in range(2)]
        h32 = sb("h32", [P, 2, UT])
        hh = sb("hh", [P, 4, 2, UT], R)
        ps_z = c.enter_context(nc.psum_tensor("ff_ps_z", [P, KD, S], F32))
        ps_h = c.enter_context(nc.psum_tensor("ff_ps_h", [P, 4, S], F32))
        ps_o = c.enter_context(nc.psum_tensor("ff_ps_o", [P, 2, S], F32))

        w_loaded = sem("w_loaded")
        w_rounded, w_split = sem("w_rounded"), sem("w_split")
        small = [sem(f"small{k}") for k in range(2)]
        gathered = [sem(f"gathered{u}") for u in range(NB)]
        scattered = [sem(f"scattered{u}") for u in range(NB)]
        z_full, z_read, n_hi, n_lo = sem("z_full"), sem("z_read"), sem("n_hi"), sem("n_lo")
        up_full, gelu_done, h_hi, h_lo, down_done = [sem(x) for x in ("up_full", "gelu_done", "h_hi", "h_lo", "down_done")]
        gather_begun, scatter_begun, reload = sem("gather_begun"), sem("scatter_begun"), sem("reload")
        n32_half, biased, added = sem("n32_half"), sem("biased"), sem("added")
        G0, L0, H0, A0, SC0 = 4, 2, 4, 1, 16

        def acc(q):
            return ps_o[:, q // 2, (q % 2) * D:(q % 2 + 1) * D]

        block = c.enter_context(nc.Block())

        def each(engine_loop, body):
            if E // 2 > 1:
                with engine_loop(0, E // 2 - 1) as i:
                    body(i, False)
            body(E // 2 - 1, True)

        @block.sync
        def _(sp):
            def load(e, k, expert):
                sp.dma_start(raw1[:], a["w1"][expert].rearrange("(k p) f -> p k f", p=P)).then_inc(w_loaded, 16)
                sp.dma_start(raw2[:], a["w2"][expert].rearrange("(n p) d -> p n d", p=P)).then_inc(w_loaded, 16)
                load_small(k, expert)

            def load_small(k, expert):
                sp.dma_start(b1[k][:], a["b1"][expert]).then_inc(small[k], 16)
                sp.dma_start(b2[k][:], a["b2"][expert].unsqueeze(0).broadcast_to([P, D])).then_inc(small[k], 16)
                src = t["order"].rearrange("(e t p) o -> e p (t o)", p=P, e=E)[expert]
                sp.dma_start(idx[k][:], src, allow_slow_non_contiguous=True).then_inc(small[k], 16)

            def body(i, last):
                for k in range(2):
                    if last and k == 1:
                        break
                    e = 2 * i + k
                    sp.wait_ge(w_split, 2 * (e + 1))
                    sp.sem_inc(reload, 1)
                    for u in range(UNITS * (1 - k), UNITS * (2 - k)):
                        sp.wait_ge(scattered[u], 16 * TU * (i + k) + SC0)
                        sp.sem_inc(reload, 1)
                    load(e, 1 - k, e + 1)

            load(0, 0, 0)
            sp.sem_inc(added, A0)
            sp.sem_inc(gelu_done, G0)
            sp.sem_inc(down_done, H0)
            each(sp.Fori, body)

        @block.gpsimd
        def _(pool):
            G = nc.gpsimd

            def gather(i, u):
                i, u = i + u // NB, u % NB
                k, first = u // UNITS, (u % UNITS) * TU
                pool.wait_ge(scattered[u], 16 * TU * i + SC0)
                if u % UNITS == 0:
                    pool.wait_ge(small[k], 48 * (i + 1))
                pool.sem_inc(gather_begun, 1)
                for q in range(TU):
                    G.indirect_dma_start(rows[u][:, q], None, t["rows"],
                                         bass.IndirectOffsetOnAxis(ap=idx[k][:, first + q:first + q + 1], axis=0)
                                         ).then_inc(gathered[u], 16)

            def scatter(i, u):
                k, first = u // UNITS, (u % UNITS) * TU
                pool.wait_ge(added, NB * i + u + 1 + A0)
                pool.sem_inc(scatter_begun, 1)
                for q in range(TU):
                    G.indirect_dma_start(out_rows, bass.IndirectOffsetOnAxis(ap=idx[k][:, first + q:first + q + 1], axis=0),
                                         rows[u][:, q, D:2 * D], None).then_inc(scattered[u], 16)

            def bias(i, u):
                k = u // UNITS
                pool.wait_ge(gathered[u], 16 * TU * (i + 1))
                pool.wait_ge(small[k], 48 * (i + 1))
                G.tensor_tensor(rows[u][:, :, D:2 * D], rows[u][:, :, D:2 * D],
                                b2[k][:].unsqueeze(1).broadcast_to([P, TU, D]), ALU.add).then_inc(biased, 1)

            def rest(i, u):
                n = NB * i + u
                pool.wait_ge(n_hi, n + 1)
                par = u % 2
                G.tensor_tensor(nT[par][:, 1], n32[:], nT[par][:, 0].bitcast(F32), ALU.subtract).then_inc(n_lo, 1)

            def body(i, last):
                for u in range(NB):
                    end = last and u == NB - 1
                    if not (last and u + AHEAD >= NB):
                        gather(i, u + AHEAD)
                    bias(i, u)
                    if not end:
                        rest(i, u + 1)
                    scatter(i, u)

            for u in range(NB):
                pool.dma_start(primer[:, u:u + 1], t["order"][0:P]).then_inc(scattered[u], 16)
            for u in range(AHEAD):
                gather(0, u)
            rest(0, 0)
            each(pool.Fori, body)
            for u in range(NB):
                pool.wait_ge(scattered[u], 16 * TU * (E // 2) + SC0)

        @block.tensor
        def _(pe):
            T = nc.tensor

            def transposed(i, u):
                n = NB * i + u
                i, u = i + u // NB, u % NB
                pe.wait_ge(gathered[u], 16 * TU * (i + 1))
                if not (isinstance(n, int) and n == 0):
                    pe.wait_ge(z_read, n)
                for kd in range(KD):
                    for q in range(TU):
                        last = T.transpose(ps_z[:, kd, q * P:(q + 1) * P], rows[u][:, q, kd * P:(kd + 1) * P], t["ident"][:])
                last.then_inc(z_full, 1)

            def up(i, u, f):
                k, par = u // UNITS, u % 2
                n = NF * (NB * i + u) + f
                if f == 0:
                    pe.wait_ge(n_lo, NB * i + u + 1)
                    pe.wait_ge(w_split, 2 * (2 * i + k) + 2)
                pe.wait_ge(gelu_done, n - 3 + G0)
                dst = ps_h[:, f % 4, 0:UT]
                for kd in range(KD):
                    wt = [w1[k][:, j, kd, f * P:(f + 1) * P] for j in range(2)]
                    x = [nT[par][:, j, kd] for j in range(2)]
                    T.matmul(dst, wt[0], x[0], start=(kd == 0), stop=False)
                    T.matmul(dst, wt[0], x[1], start=False, stop=False)
                    last = T.matmul(dst, wt[1], x[0], start=False, stop=(kd == KD - 1))
                last.then_inc(up_full, 1)

            def down(i, u, f):
                k = u // UNITS
                n = NF * (NB * i + u) + f
                pe.wait_ge(h_lo, n + 1 + L0)
                if f == 0:
                    pe.wait_ge(added, NB * i + u + A0)
                for q in range(TU):
                    x = [hh[:, f % 4, j, q * P:(q + 1) * P] for j in range(2)]
                    wt = [w2[k][:, j, f] for j in range(2)]
                    for m, (xx, ww) in enumerate(((x[0], wt[0]), (x[0], wt[1]), (x[1], wt[0]))):
                        last = T.matmul(acc(q), xx, ww, start=(f == 0 and m == 0 and q % 2 == 0),
                                        stop=(f == NF - 1 and m == 2), skip_group_check=True)
                last.then_inc(down_done, 1)

            def body(i, last):
                for u in range(NB):
                    for f in range(NF):
                        up(i, u, f)
                        if f >= 2:
                            down(i, u, f - 2)
                        if f == 4 and not (last and u == NB - 1):
                            transposed(i, u + 1)
                    down(i, u, NF - 2)
                    down(i, u, NF - 1)

            transposed(0, 0)
            each(pe.Fori, body)

        @block.scalar
        def _(act):
            A = nc.scalar

            def normed(i, u):
                n = NB * i + u
                par = u % 2
                act.wait_ge(z_full, n + 1)
                if not (isinstance(n, int) and n == 0):
                    act.wait_ge(n_lo, n)
                for kd in range(KD):
                    last = A.activation(n32[:, kd], ps_z[:, kd, 0:UT], ACT.Identity, bias=t["ffn_b"][:, kd:kd + 1],
                                        scale=t["ffn_g"][:, kd:kd + 1])
                    last.then_inc(z_read if kd else n32_half, 1)
                act.wait_ge(n32_half, n + 1)
                act.wait_ge(z_read, n + 1)
                A.copy(nT[par][:, 0], n32[:]).then_inc(n_hi, 1)

            def body(i, last):
                for u in range(NB):
                    k = u // UNITS
                    for f in range(NF):
                        n = NF * (NB * i + u) + f
                        act.wait_ge(up_full, n + 1)
                        if f == 0 and u % UNITS == 0:
                            act.wait_ge(small[k], 48 * (i + 1))
                        act.wait_ge(h_lo, n - 1 + L0)
                        A.activation(h32[:, f % 2], ps_h[:, f % 4, 0:UT], ACT.Gelu_apprx_tanh,
                                     bias=b1[k][:, f:f + 1]).then_inc(gelu_done, 1)
                        if f == 4 and not (last and u == NB - 1):
                            normed(i, u + 1)

            normed(0, 0)
            each(act.Fori, body)

        @block.vector
        def _(dve):
            V = nc.vector

            def convert(e, k, part):
                dst, src = ((w1, raw1), (w2, raw2))[part // 2]
                if part == 0:
                    dve.wait_ge(w_loaded, 32 * (e + 1))
                if part % 2 == 0:
                    V.tensor_copy(dst[k][:, 0], src[:]).then_inc(w_rounded, 1)
                else:
                    dve.wait_ge(w_rounded, 2 * e + part // 2 + 1)
                    V.tensor_tensor(dst[k][:, 1], src[:], dst[k][:, 0].bitcast(F32), ALU.subtract).then_inc(w_split, 1)

            def body(i, last):
                for u in range(NB):
                    k = u // UNITS
                    for f in range(NF):
                        n = NF * (NB * i + u) + f
                        dve.wait_ge(gelu_done, n + 1 + G0)
                        dve.wait_ge(down_done, n - 3 + H0)
                        V.tensor_copy(hh[:, f % 4, 0], h32[:, f % 2]).then_inc(h_hi, 1)
                        dve.wait_ge(h_hi, n + 1)
                        V.tensor_tensor(hh[:, f % 4, 1], h32[:, f % 2], hh[:, f % 4, 0].bitcast(F32),
                                        ALU.subtract).then_inc(h_lo, 1)
                        if u % UNITS == UNITS - 1 and 3 <= f <= 6 and not (last and k == 1):
                            dve.wait_ge(added, NB * i + u + A0)
                            convert(2 * i + k + 1, 1 - k, f - 3)
                    dve.wait_ge(down_done, NF * (NB * i + u + 1) + H0)
                    dve.wait_ge(biased, NB * i + u + 1)
                    if TU == 4:
                        o = rows[u][:, :, D:2 * D]
                        last_add = V.tensor_tensor(o, ps_o[:].rearrange("p i (q d) -> p (i q) d", q=2), o, ALU.add)
                    else:
                        for q in range(TU):
                            o = rows[u][:, q, D:2 * D]
                            last_add = V.tensor_tensor(o, acc(q), o, ALU.add)
                    last_add.then_inc(added, 1)

            dve.sem_inc(h_lo, L0)
            for part in range(4):
                convert(0, 0, part)
            each(dve.Fori, body)


def build(nc, B, a, out, stages=4):
    T = B * S
    NT = T // P
    rows = nc.dram_tensor("rows_scratch", (T, 2 * D), F32).ap()
    order = nc.dram_tensor("order_scratch", (T, 1), I32).ap()
    with ExitStack() as c:
        def sb(name, shape, dt=F32):
            return c.enter_context(nc.sbuf_tensor(name, shape, dt))

        t = {
            "x": a["x"],
            "rows": rows,
            "rows_by_seq": rows.rearrange("(b t p) c -> b p t c", p=P, t=TQ),
            "order": order,
            "out": out,
            "ident": sb("ident", [P, P]),
            "ones": sb("ones", [P, P]),
            "ffn_g": sb("ffn_g", [P, KD]),
            "ffn_b": sb("ffn_b", [P, KD]),
        }
        scores_stack = c.enter_context(ExitStack())

        def sc(name, shape, dt=F32):
            return scores_stack.enter_context(nc.sbuf_tensor(name, shape, dt))

        t["scores"] = sc("scores", [P, E, NT])
        t["centT"] = sc("centT", [P, KD, E])
        t["before"] = sc("before", [P, P])
        t["token_ids"] = sc("token_ids", [P, NT], I32)
        t["cand_bits"] = sc("cand_bits", [P, len(SHIFTS), CANDS], I32)
        loaded = c.enter_context(nc.semaphore("consts_loaded"))
        with nc.Block() as block:
            @block.sync
            def _(sp):
                loads = [
                    (t["ident"][:], a["ident"]),
                    (t["before"][:], a["before"]),
                    (t["ones"][:], a["ones"]),
                    (t["ffn_g"][:], a["ffn_g"]),
                    (t["ffn_b"][:], a["ffn_b"]),
                    (t["centT"][:], a["centT"].rearrange("(k p) e -> p k e", p=P)),
                    (t["token_ids"][:], a["token_ids"]),
                    (t["cand_bits"][:], a["cand_bits"]),
                ]
                for dst, src in loads:
                    sp.dma_start(dst, src).then_inc(loaded, 16)
                sp.wait_ge(loaded, 16 * len(loads))
        layer_norm_stage(nc, t, B)
        if stages >= 2:
            routing_stage(nc, t, B)
        scores_stack.close()
        if stages >= 3:
            attention_stage(nc, t, a, B)
        if stages >= 4:
            ffn_stage(nc, t, a, B)


def constants(B):
    NT = B * S // P
    p = np.arange(P)
    rounds = np.array([[c << s if (c << s) < 2**31 else 0 for c in range(1, CANDS + 1)] for s in SHIFTS], np.int64).astype(np.int32)
    inv_freq = 1.0 / 10000.0 ** (np.arange(0, DH, 2, dtype=np.float32) / DH)
    freqs = np.outer(np.arange(S, dtype=np.float32), inv_freq)
    cos = np.concatenate([np.cos(freqs), np.cos(freqs)], -1)[:, ::2]
    sin = np.concatenate([np.sin(freqs), np.sin(freqs)], -1)[:, ::2]
    pair = (p % DH) // 2
    sign = np.where(p % 2 == 0, -1.0, 1.0).astype(np.float32)
    head_tile = np.arange(MROWS)
    return {
        "ident": np.eye(P, dtype=np.float32),
        "before": (p[:, None] < p[None, :]).astype(np.float32),
        "ones": np.ones((P, P), np.float32),
        "token_ids": (np.arange(NT)[None, :] * P + p[:, None]).astype(np.int32),
        "cand_bits": np.broadcast_to(rounds, (P, len(SHIFTS), CANDS)).copy(),
        "cos": np.ascontiguousarray(cos[:, pair].T.astype(np.float32)),
        "sin": np.ascontiguousarray((sin[:, pair].T * sign[:, None]).astype(np.float32)),
        "own_tile": np.ascontiguousarray(np.eye(MROWS, dtype=np.float32)),
    }


def arrays_of(inputs):
    i = {k: np.asarray(v) for k, v in inputs.items()}
    cc = np.ascontiguousarray
    B = i["L0_attn_x"].shape[0]

    def columns(v):
        return cc(v.reshape(-1, P).T)

    swap = np.arange(H * DH).reshape(-1, 2)[:, ::-1].ravel()
    return {
        "x": cc(i["L0_attn_x"]),
        "wdqT": cc(i["L0_attn_w_down_q"].T), "wdkvT": cc(i["L0_attn_w_down_kv"].T),
        "wq": cc(np.stack([i["L0_attn_w_up_q"].T, i["L0_attn_w_up_q"][swap].T], 1)),
        "wk": cc(np.stack([i["L0_attn_w_up_k"].T, i["L0_attn_w_up_k"][swap].T], 1)),
        "wv": cc(i["L0_attn_w_up_v"].T), "woT": cc(i["L0_attn_w_out"].T),
        "attn_g": columns(i["L0_attn_ln_scale"]), "attn_b": columns(i["L0_attn_ln_bias"]),
        "centT": cc(i["L0_ffn_centroids"].T), "ffn_g": columns(i["L0_ffn_ln_g"]), "ffn_b": columns(i["L0_ffn_ln_b"]),
        "w1": cc(i["L0_ffn_w1"]), "b1": cc(i["L0_ffn_b1"].reshape(E, NF, P).transpose(0, 2, 1)), "w2": cc(i["L0_ffn_w2"]), "b2": cc(i["L0_ffn_b2"]),
        **constants(B),
    }


def kernel(**inputs):
    import concourse.bacc as bacc
    from concourse.bass_utils import run_bass_kernel_spmd

    arrays = arrays_of(inputs)
    B = arrays["x"].shape[0]
    nc = bacc.Bacc("TRN2", target_bir_lowering=False, num_devices=1)
    a = {n: nc.dram_tensor("in_" + n, v.shape, mybir.dt.from_np(v.dtype), kind="ExternalInput").ap() for n, v in arrays.items()}
    out = nc.dram_tensor("out", (B, S, D), F32, kind="ExternalOutput").ap()
    build(nc, B, a, out)
    got = run_bass_kernel_spmd(nc, [{"in_" + n: v for n, v in arrays.items()}], core_ids=[0])
    return got.results[0]["out"]
```

```python
from contextlib import ExitStack

import numpy as np

import concourse.bass as bass
from concourse import mybir

F32 = mybir.dt.float32
F32R = mybir.dt.float32r
I32 = mybir.dt.int32
ACT = mybir.ActivationFunctionType
ALU = mybir.AluOpType
AX = mybir.AxisListType
RADD = bass.bass_isa.ReduceOp.add

P = 128
S = 512
D = 256
KD = D // P
H = 16
DH = 64
L = 128
PAIRS = H // 2
TQ = S // P
E = 8
FF = 1024
NF = FF // P
EPS = 1e-5
SCALE = 1.0 / 8.0
BIG = -3.0e38
SHIFTS = [28, 25, 22, 19, 16, 13, 10, 7, 4, 1, 0]
CANDS = 7
MROWS = 2 * TQ


def layer_norm_stage(nc, t, a, B):
    sem = {}
    with ExitStack() as c:
        def sb(name, shape, dt=F32):
            return c.enter_context(nc.sbuf_tensor(name, shape, dt))

        for n in (*(f"{w}{k}" for w in ("x_loaded", "stored") for k in range(4)), "stats_ready", "aggr_ready", "rows_ready", "z_ready", "base_ready",
                  "zt_full", "norm_ready", "score_full", "score_copied", "tile_full", "tile_copied", "pool_step", "passed"):
            sem[n] = c.enter_context(nc.semaphore("ln_" + n))
        GB = min(4, B)
        x = sb("ln_x", [P, GB, TQ, D])
        st = sb("ln_stats", [P, GB, TQ, 6])
        mv = sb("ln_mv", [P, GB, TQ, 2])
        tmp = sb("ln_tmp", [P, 8, GB, TQ])
        rows = sb("ln_rows", [P, 3, GB, TQ])
        zb = sb("ln_zb", [P, GB, TQ, 2 * D])
        normT = sb("ln_normT", [P, 2, KD, S])
        scoreT = sb("ln_scoreT", [E, 2, S])
        ps_z = c.enter_context(nc.psum_tensor("ln_ps_z", [P, 2, KD, S], F32))
        ps_s = c.enter_context(nc.psum_tensor("ln_ps_s", [E, 2, S], F32))
        ps_t = c.enter_context(nc.psum_tensor("ln_ps_t", [P, 2, S], F32))
        raw = {n: sb("raw_" + n, s) for n, s in
               (("wq", [P, 2, H * DH]), ("wk", [P, 2, H * DH]), ("wv", [P, H * DH]), ("wd", [P, KD, 2, L]))}
        loads = [
            (raw["wq"][:], a["wq"]), (raw["wk"][:], a["wk"]), (raw["wv"][:], a["wv"]),
            (raw["wd"][:, :, 0], a["wdqT"].rearrange("(k p) l -> p k l", p=P)),
            (raw["wd"][:, :, 1], a["wdkvT"].rearrange("(k p) l -> p k l", p=P)),
            (t["wo"][:], a["woT"].rearrange("(h p) d -> p h d", p=P)),
            (t["cos"][:], a["cos"]), (t["sin"][:], a["sin"]), (t["own"][:], a["own_tile"]),
            (t["gb"][:, 0], a["attn_g"]), (t["gb"][:, 1], a["attn_b"]),
        ]
        weights_loaded, weights_rounded, weights_split = [
            c.enter_context(nc.semaphore("weights_" + n)) for n in ("loaded", "rounded", "split")]
        block = c.enter_context(nc.Block())
        SLOT0 = 2

        def each(engine, body):
            if B // GB > 1:
                with engine.Fori(0, B // GB - 1) as i:
                    body(i, False)
            body(B // GB - 1, True)

        @block.sync
        def _(sp):
            def load(i, k):
                sp.dma_start(x[:, k], t["x"][GB * i + k].rearrange("(t p) d -> p t d", p=P)).then_inc(sem[f"x_loaded{k}"], 16)

            def body(i, last):
                for k in range(GB):
                    sp.wait_ge(sem["z_ready"], GB * i + k + 1)
                    sp.sem_inc(sem["passed"], 1)
                    sp.wait_ge(sem["base_ready"], GB * i + k + 1)
                    sp.sem_inc(sem["passed"], 1)
                    if not last:
                        load(i + 1, k)
                for k in range(GB):
                    sp.dma_start(t["rows_by_seq"][GB * i + k], zb[:, k]).then_inc(sem[f"stored{k}"], 16)

            for k in range(GB):
                load(0, k)
            for dst, src in loads:
                sp.dma_start(dst, src).then_inc(weights_loaded, 16)
            each(sp, body)
            for k in range(GB):
                sp.wait_ge(sem[f"stored{k}"], 16 * (B // GB) + 16)

        @block.vector
        def _(dve):
            def stats(i):
                for k in range(GB):
                    dve.wait_ge(sem[f"x_loaded{k}"], 16 * i + 16)
                    for q in range(TQ):
                        last = nc.vector.bn_stats(st[:, k, q], x[:, k, q])
                last.then_inc(sem["stats_ready"], 1)
                dve.wait_ge(sem["stats_ready"], i + 1)
                dve.sem_inc(sem["passed"], 1)
                for k in range(GB):
                    for q in range(TQ):
                        last = nc.vector.bn_aggr(mv[:, k, q], st[:, k, q])
                last.then_inc(sem["aggr_ready"], 1)

            names = ("wq", "wk", "wv", "wd")

            def round_weights():
                dve.wait_ge(weights_loaded, 16 * len(loads))
                for name in names:
                    nc.vector.tensor_copy(t[name][:, 0], raw[name][:]).then_inc(weights_rounded, 1)

            def split_weights():
                for n, name in enumerate(names):
                    dve.wait_ge(weights_rounded, n + 1)
                    nc.vector.tensor_tensor(t[name][:, 1], raw[name][:], t[name][:, 0].bitcast(F32), ALU.subtract).then_inc(weights_split, 1)

            def body(i, last_group):
                if last_group:
                    round_weights()
                dve.wait_ge(sem["rows_ready"], i + 1)
                for k in range(GB):
                    dve.wait_ge(sem[f"stored{k}"], 16 * i + 16)
                    for q in range(TQ):
                        last = nc.vector.tensor_scalar(zb[:, k, q, 0:D], x[:, k, q], mv[:, k, q, 0:1],
                                                       rows[:, 0, k, q:q + 1], ALU.subtract, ALU.mult)
                    last.then_inc(sem["z_ready"], 1)
                if last_group:
                    split_weights()
                else:
                    stats(i + 1)
                for k in range(GB + 1):
                    if k < GB:
                        dve.wait_ge(sem["score_full"], GB * i + k + 1 + SLOT0)
                        nc.vector.tensor_copy(scoreT[:, k % 2], ps_s[:, k % 2]).then_inc(sem["score_copied"], 1)
                    if k:
                        j = k - 1
                        dve.wait_ge(sem["tile_full"], GB * i + j + 1)
                        nc.vector.tensor_copy(
                            t["scores"][:, :, bass.ds((GB * i + j) * TQ, TQ)],
                            ps_t[:, j % 2, 0:TQ * E].rearrange("p (t e) -> p e t", e=E)).then_inc(sem["tile_copied"], 1)

            stats(0)
            each(dve, body)

        @block.gpsimd
        def _(pool):
            nc.gpsimd.memset(tmp[:, 7], -0.5).then_inc(sem["pool_step"], 1)
            for k in range(GB):
                pool.sem_inc(sem[f"stored{k}"], 16)
            with pool.Fori(0, B // GB) as i:
                pool.wait_ge(sem["aggr_ready"], i + 1)
                mean = mv[:, :, :, 0]
                var = mv[:, :, :, 1]
                steps = [
                    lambda: nc.gpsimd.tensor_scalar(tmp[:, 0], var, EPS, None, ALU.add),
                    lambda: nc.gpsimd.tensor_tensor(tmp[:, 1], tmp[:, 0], tmp[:, 7], ALU.pow),
                    lambda: nc.gpsimd.tensor_tensor(tmp[:, 2], var, tmp[:, 1], ALU.mult),
                    lambda: nc.gpsimd.tensor_tensor(tmp[:, 3], tmp[:, 2], tmp[:, 1], ALU.mult),
                    lambda: nc.gpsimd.tensor_scalar(tmp[:, 4], tmp[:, 3], EPS, None, ALU.add),
                    lambda: nc.gpsimd.tensor_tensor(tmp[:, 5], tmp[:, 4], tmp[:, 7], ALU.pow),
                    lambda: nc.gpsimd.tensor_tensor(rows[:, 0], tmp[:, 5], tmp[:, 1], ALU.mult),
                    lambda: nc.gpsimd.tensor_scalar(rows[:, 1], tmp[:, 1], 2.0, 1.0, ALU.mult, ALU.add),
                    lambda: nc.gpsimd.tensor_tensor(tmp[:, 6], mean, tmp[:, 1], ALU.mult),
                ]
                for j, step in enumerate(steps):
                    pool.wait_ge(sem["pool_step"], 9 * i + j + 1)
                    pool.sem_inc(sem["passed"], 1)
                    step().then_inc(sem["pool_step"], 1)
                pool.wait_ge(sem["pool_step"], 9 * i + 10)
                pool.sem_inc(sem["passed"], 1)
                nc.gpsimd.tensor_scalar(rows[:, 2], tmp[:, 6], -2.0, None, ALU.mult).then_inc(sem["rows_ready"], 1)

        @block.scalar
        def _(act):
            with act.Fori(0, B // GB) as i:
                act.wait_ge(sem["rows_ready"], i + 1)
                for j in range(GB + 1):
                    if j < GB:
                        act.wait_ge(sem[f"stored{j}"], 16 * i + 16)
                        for q in range(TQ):
                            last = nc.scalar.activation(zb[:, j, q, D:2 * D], x[:, j, q], ACT.Identity,
                                                        bias=rows[:, 2, j, q:q + 1], scale=rows[:, 1, j, q:q + 1])
                        last.then_inc(sem["base_ready"], 1)
                    if j:
                        k = j - 1
                        act.wait_ge(sem["zt_full"], GB * i + k + 1)
                        act.wait_ge(sem["score_full"], GB * i + k + 1)
                        for kd in range(KD):
                            last = nc.scalar.activation(normT[:, k % 2, kd], ps_z[:, k % 2, kd], ACT.Identity,
                                                        bias=t["ffn_b"][:, kd:kd + 1], scale=t["ffn_g"][:, kd:kd + 1])
                        last.then_inc(sem["norm_ready"], 1)

        @block.tensor
        def _(pe):
            for name in ("norm_ready", "score_copied", "tile_copied", "score_full"):
                pe.sem_inc(sem[name], SLOT0)
            with pe.Fori(0, B // GB) as i:
                for j in range(GB + 2):
                    if j < GB:
                        n = GB * i + j
                        pe.wait_ge(sem["z_ready"], n + 1)
                        pe.wait_ge(sem["norm_ready"], n + 1)
                        for kd in range(KD):
                            for q in range(TQ):
                                last = nc.tensor.transpose(ps_z[:, j % 2, kd, q * P:(q + 1) * P],
                                                           zb[:, j, q, kd * P:(kd + 1) * P], t["ident"][:])
                        last.then_inc(sem["zt_full"], 1)
                    if 0 <= j - 1 < GB:
                        k = j - 1
                        n = GB * i + k
                        pe.wait_ge(sem["norm_ready"], n + 1 + SLOT0)
                        pe.wait_ge(sem["score_copied"], n + 1)
                        for kd in range(KD):
                            last = nc.tensor.matmul(ps_s[:, k % 2], t["centT"][:, kd], normT[:, k % 2, kd],
                                                    start=(kd == 0), stop=(kd == KD - 1))
                        last.then_inc(sem["score_full"], 1)
                    if 0 <= j - 2 < GB:
                        k = j - 2
                        n = GB * i + k
                        pe.wait_ge(sem["score_copied"], n + 1 + SLOT0)
                        pe.wait_ge(sem["tile_copied"], n + 1)
                        pe.sem_inc(sem["passed"], 1)
                        for q in range(TQ):
                            last = nc.tensor.transpose(ps_t[:, k % 2, q * E:(q + 1) * E],
                                                       scoreT[:, k % 2, q * P:(q + 1) * P], t["ident"][0:E, 0:E])
                        last.then_inc(sem["tile_full"], 1)


def attention_stage(nc, t, a, B):
    R = F32R
    NT = B * S // P
    C = B * S // E
    assert B == 2 * E
    with ExitStack() as c:
        def sb(name, shape, dt=F32):
            return c.enter_context(nc.sbuf_tensor("at_" + name, shape, dt))

        def sem(name):
            return c.enter_context(nc.semaphore("at_" + name))

        wq, wk, wv, wd, wo, cos, sin, own, gb = [t[n] for n in ("wq", "wk", "wv", "wd", "wo", "cos", "sin", "own", "gb")]
        zr = sb("zr", [P, TQ, D])
        h32 = sb("h32", [P, 2, S])
        hs = sb("hs", [P, 2, KD, S], R)
        cl = sb("cl", [P, 2, 2, S], R)
        V = sb("V", [P, TQ, H * DH])
        rot = sb("rot", [P, 4, S])
        qr = sb("qr", [P, S])
        kr = sb("kr", [P, S])
        kA = sb("kA", [P, 2, 2, S], R)
        kB = sb("kB", [P, 2, 2, S], R)
        qC = sb("qC", [P, 2, 2, S], R)
        qD = sb("qD", [P, 2, 2, S], R)
        mx = sb("mx", [P, MROWS])
        probs = sb("probs", [P, 2, TQ, 2, S])
        psum_k = sb("psum_k", [P, 2, S])
        den_t = sb("den_t", [P, S])
        rec_col = sb("rec_col", [P, S // 32])
        rec = sb("rec", [P, S])
        oT = sb("oT", [P, PAIRS, S])
        v = sb("rt_v", [P, NT])
        avail = sb("rt_avail", [P, NT])
        pen = sb("rt_pen", [P, NT])
        w = sb("rt_work", [P, 10, NT])
        ge = sb("rt_ge", [P, CANDS, NT])
        cand = sb("rt_cand", [P, CANDS], I32)
        cur = sb("rt_cur", [P, 2], I32)
        step = sb("rt_step", [P, 1], I32)
        cnt = sb("rt_cnt", [P, CANDS])
        tot = sb("rt_tot", [P, CANDS])
        flags = sb("rt_flags", [P, CANDS])
        one = sb("rt_one", [P, 8])
        nrem = sb("rt_nrem", [P, 2])
        pos = sb("rt_pos", [P, NT])
        posi = sb("rt_posi", [P, NT], I32)
        ring = [c.enter_context(nc.psum_tensor(f"at_ring{i}", [P, 2, S], F32)) for i in range(2)]
        mb = c.enter_context(nc.psum_tensor("at_maxima", [P, 2, S], F32))
        po = c.enter_context(nc.psum_tensor("at_out", [P, S], F32))
        xb = c.enter_context(nc.psum_tensor("at_mixed", [P, S], F32))

        ring_full, ring_read = sem("ring_full"), sem("ring_read")
        x_full, x_read = sem("x_full"), sem("x_read")
        m_full, m_read = sem("m_full"), sem("m_read")
        mt_full, m_rows = sem("mt_full"), sem("m_rows")
        pv_full, o_done = sem("pv_full"), sem("o_done")
        out_full, out_done = sem("out_full"), sem("out_done")
        qr_ready, kr_ready = sem("qr_ready"), sem("kr_ready")
        hi_ready, kb_ready = sem("hi_ready"), sem("kb_ready")
        alo_ready, qlo_ready = sem("alo_ready"), sem("qlo_ready")
        summed = sem("summed")
        rec_step = sem("rec_step")
        h32_ready, hhi_ready, hlo_ready = sem("h32_ready"), sem("hhi_ready"), sem("hlo_ready")
        c32_ready, chi_ready, clo_ready = sem("c32_ready"), sem("chi_ready"), sem("clo_ready")
        z_loaded, res_loaded, res_stored, reload = sem("z_loaded"), sem("res_loaded"), sem("res_stored"), sem("reload")
        rt_step, rt_asked, rt_count, rt_total, rt_list, rt_rows, rt_scattered = [
            sem("rt_" + n) for n in ("step", "asked", "count", "total", "list", "rows", "scattered")]
        start = sem("start")

        PV0, SUM0, O0, OUT0, STORED0 = 2, 6, 1, 1, 16
        PER_SEQ = TQ + PAIRS * TQ + 2

        def ring_local(b, kind, p=0, kt=0):
            last = isinstance(b, int) and b == B - 1
            if kind == "V":
                return kt
            if kind == "z":
                return TQ + 5 * TQ
            if kind == "c":
                return TQ + 6 * TQ + 1
            return TQ + TQ * p + kt + (0 if last else (p >= 5) + (p >= 6))

        def ring_at(b, kind, p=0, kt=0):
            return 2 + PER_SEQ * b + ring_local(b, kind, p, kt)

        def x_order(kind):
            order = []
            for p in range(PAIRS):
                order += [("den", p - 1)] if p else []
                order += [(w, p + 2) for w in ("qA", "qB", "kA", "kB")] if p + 2 < PAIRS or kind != "odd_last" else []
                order += [("list", j) for j in range(2) if LIST_AT.get((kind, j)) == p]
            return order + [("den", PAIRS - 1)]

        LIST_AT = {("odd", 0): 4, ("odd", 1): 5, ("even_last", 1): 0}
        KINDS = ("even", "odd", "even_last", "odd_last")
        X = {kind: {u: n for n, u in enumerate(x_order(kind))} for kind in KINDS}
        X_EVEN, X_ODD, X_EVEN_LAST = [len(X[kind]) for kind in KINDS[:3]]

        def x_uses(i, odd, last):
            before = 8 + (X_EVEN + X_ODD) * i + ((X_EVEN_LAST if last else X_EVEN) if odd else 0)
            return before, ("odd" if odd else "even") + ("_last" if last else "")

        def x_at(xs, use):
            return xs[0] + X[xs[1]][use]

        ROUNDS = len(SHIFTS)
        SUMS = ROUNDS + 2
        assert SUMS - 1 == PAIRS + LIST_AT["odd", 0]

        def each_pair(engine, body):
            with engine.Fori(0, E - 1) as i:
                body(i, 0, False)
                body(i, 1, False)
            body(E - 1, 0, True)
            body(E - 1, 1, True)

        WHAT = {"qA": (wq, 0, 0), "qB": (wq, 1, 0), "kA": (wk, 0, 1), "kB": (wk, 1, 1)}

        block = c.enter_context(nc.Block())

        @block.sync
        def _(sp):
            def load_z(b):
                sp.dma_start(zr[:], t["rows_by_seq"][b][:, :, 0:D]).then_inc(z_loaded, 16)

            def body(i, odd, last_two):
                b, last = 2 * i + odd, last_two and odd == 1
                if not last:
                    sp.wait_ge(res_stored, 16 * b + STORED0)
                    sp.sem_inc(reload, 1)
                    load_z(b + 1)
                    sp.wait_ge(ring_full, ring_at(b, "z") + 1)
                else:
                    sp.wait_ge(res_stored, 16 * b + STORED0)
                sp.sem_inc(reload, 1)
                sp.dma_start(zr[:], t["rows_by_seq"][b][:, :, D:2 * D]).then_inc(res_loaded, 16)
                sp.wait_ge(out_done, b + 1 + OUT0)
                sp.dma_start(t["rows_by_seq"][b][:, :, D:2 * D], zr[:]).then_inc(res_stored, 16)

            load_z(0)
            sp.wait_ge(ring_full, 1)
            sp.sem_inc(res_stored, STORED0)
            each_pair(sp, body)
            sp.wait_ge(res_stored, 16 * B + STORED0)

        @block.tensor
        def _(pe):
            T = nc.tensor

            def mm3(dst, w, x, first, last):
                T.matmul(dst, w[0], x[0], start=first, stop=False)
                T.matmul(dst, w[0], x[1], start=False, stop=False)
                return T.matmul(dst, w[1], x[0], start=False, stop=last)

            def ring_slot(n, local):
                if not (isinstance(n, int) and n < 2):
                    pe.wait_ge(ring_read, n - 1)
                return ring[local % 2]

            def transpose_z(b, n):
                pe.wait_ge(z_loaded, 16 * b + 16)
                slot = ring_slot(n, 0)
                for kd in range(KD):
                    for q in range(TQ):
                        last = T.transpose(slot[:, kd, q * P:(q + 1) * P], zr[:, q, kd * P:(kd + 1) * P], t["ident"][:])
                last.then_inc(ring_full, 1)

            def latents(b, n):
                pe.wait_ge(hlo_ready, b + 1)
                pe.wait_ge(hhi_ready, b + 1)
                slot = ring_slot(n, 1)
                for w in range(2):
                    for kd in range(KD):
                        last = mm3(slot[:, w], [wd[:, i, kd, w] for i in range(2)], [hs[:, i, kd] for i in range(2)],
                                   kd == 0, kd == KD - 1)
                last.then_inc(ring_full, 1)

            def values(b):
                for kt in range(TQ):
                    slot = ring_slot(ring_at(b, "V", 0, kt), kt)
                    for n in range(2):
                        last = mm3(slot[:, n], [cl[:, i, 1, kt * P:(kt + 1) * P] for i in range(2)],
                                   [wv[:, i, n * S:(n + 1) * S] for i in range(2)], True, True)
                    last.then_inc(ring_full, 1)

            def project(n, what, p, seq):
                if n is not None:
                    pe.wait_ge(x_read, n)
                if p % PAIRS == 0 and what == "qA":
                    pe.wait_ge(clo_ready, seq + 1)
                    pe.wait_ge(chi_ready, seq + 1)
                w, swap, which = WHAT[what]
                cols = slice((p % PAIRS) * P, (p % PAIRS + 1) * P)
                mm3(xb[:], [w[:, i, swap, cols] for i in range(2)], [cl[:, i, which] for i in range(2)],
                    True, True).then_inc(x_full, 1)

            def maxima(g, p, j, b=None):
                par, head = p % 2, j // 2
                if not (isinstance(g, int) and g == 0 and j == 0):
                    pe.wait_ge(m_read, 4 * g + j)
                if j == 0 and p:
                    pe.wait_ge(m_rows, g)
                if j == 0 and p == 1:
                    pe.wait_ge(out_done, b + OUT0)
                if j % 2 == 0:
                    pe.wait_ge(alo_ready, 2 * g + head + 1)
                for i in range(2):
                    q = 2 * (j % 2) + i
                    last = T.matmul(mb[:, i], qC[:, par, head, q * P:(q + 1) * P], kA[:, par, head], start=True, stop=True)
                last.then_inc(m_full, 1)

            def maxima_rows(g):
                pe.wait_ge(m_read, 4 * g + 4)
                T.transpose(mb[0:MROWS, 0, 0:P], mx[:], t["ident"][:]).then_inc(mt_full, 1)

            def scores(b, g, p, kt):
                par = p % 2
                n = ring_at(b, "S", p, kt)
                slot = ring_slot(n, ring_local(b, "S", p, kt))
                if kt == 0:
                    pe.wait_ge(m_rows, g + 1)
                    pe.wait_ge(qlo_ready, 2 * g + 2)
                    pe.wait_ge(kb_ready, g + 1)
                keys = slice(kt * P, (kt + 1) * P)
                for head in range(2):
                    T.matmul(slot[:, head], kA[:, par, head, keys], qC[:, par, head], start=True, stop=False)
                    last = T.matmul(slot[:, head], kB[0:DH + MROWS, par, head, keys], qD[0:DH + MROWS, par, head],
                                    start=False, stop=True)
                last.then_inc(ring_full, 1)

            def times_v(b, g, p, kt):
                if kt == 0:
                    pe.wait_ge(o_done, g + O0)
                pe.wait_ge(ring_read, ring_at(b, "S", p, kt) + 1)
                for head in range(2):
                    h = 2 * p + head
                    last = T.matmul(po[head * DH:(head + 1) * DH], V[:, kt, h * DH:(h + 1) * DH],
                                    probs[:, p % 2, kt, head], start=(kt == 0), stop=(kt == TQ - 1))
                if kt == TQ - 1:
                    last.then_inc(pv_full, 1)

            def denominators(xs, g, p):
                pe.wait_ge(x_read, x_at(xs, ("den", p)))
                pe.wait_ge(summed, 3 * g + 3 + SUM0)
                for head in range(2):
                    last = T.matmul(xb[head * DH:(head + 1) * DH], t["ones"][:, 0:DH], psum_k[:, head], start=True, stop=True)
                last.then_inc(x_full, 1)

            def earlier(xs, e, j):
                pe.wait_ge(x_read, x_at(xs, ("list", j)))
                pe.wait_ge(rt_list, 2 * e + (1 if xs[1] == "even_last" else j + 1))
                T.matmul(xb[:, 0:NT], t["before"][:], w[:, 8 + j], start=True, stop=True)
                T.matmul(xb[:, NT:2 * NT], t["ones"][:], w[:, 8 + j], start=True, stop=True).then_inc(x_full, 1)

            def out_pair(b, p):
                pe.wait_ge(o_done, PAIRS * b + p + 1 + O0)
                for q in range(TQ):
                    last = T.matmul(mb[:, q // 2, (q % 2) * D:(q % 2 + 1) * D], oT[:, p, q * P:(q + 1) * P], wo[:, p],
                                    start=(p == 0 and q % 2 == 0), stop=(p == PAIRS - 1), skip_group_check=True)
                if p == PAIRS - 1:
                    last.then_inc(out_full, 1)

            def body(i, odd, last_two):
                b, last = 2 * i + odd, last_two and odd == 1
                xs = x_uses(i, odd, last_two)
                values(b)
                for p in range(PAIRS):
                    g = PAIRS * b + p
                    prev = (b, g - 1, p - 1)
                    ahead = not last or p + 2 < PAIRS
                    nxt = not last or p + 1 < PAIRS

                    def proj(what):
                        if ahead:
                            project(x_at(xs, (what, p + 2)), what, p + 2, b + (p + 2) // PAIRS)

                    def mxs(j):
                        if nxt:
                            maxima(g + 1, p + 1, j, b)

                    if p:
                        times_v(*prev, 0)
                        times_v(*prev, 1)
                    scores(b, g, p, 0)
                    scores(b, g, p, 1)
                    if p:
                        denominators(xs, g - 1, p - 1)
                    mxs(0)
                    proj("qA")
                    if p:
                        times_v(*prev, 2)
                    mxs(1)
                    proj("qB")
                    scores(b, g, p, 2)
                    mxs(2)
                    proj("kA")
                    if p:
                        times_v(*prev, 3)
                    mxs(3)
                    scores(b, g, p, 3)
                    proj("kB")
                    if nxt:
                        maxima_rows(g + 1)
                    if p == 4 and not last:
                        transpose_z(b + 1, ring_at(b, "z"))
                    if p == 5 and not last:
                        latents(b + 1, ring_at(b, "c"))
                    for j in range(2):
                        if LIST_AT.get((xs[1], j)) == p:
                            earlier(xs, i, j)
                g = PAIRS * b + PAIRS - 1
                pe.wait_ge(m_rows, g + 1 if last else g + 2)
                for p in range(PAIRS - 2):
                    out_pair(b, p)
                for kt in range(TQ):
                    times_v(b, g, PAIRS - 1, kt)
                denominators(xs, g, PAIRS - 1)
                for p in (PAIRS - 2, PAIRS - 1):
                    out_pair(b, p)

            pe.wait_ge(start, 1)
            transpose_z(0, 0)
            latents(0, 1)
            for p in range(2):
                for j, what in enumerate(("qA", "qB", "kA", "kB")):
                    project(4 * p + j if p + j else None, what, p, 0)
            for j in range(4):
                maxima(0, 0, j)
            maxima_rows(0)
            each_pair(pe, body)

        @block.scalar
        def _(act):
            A = nc.scalar

            def normed(b, n):
                act.wait_ge(ring_full, n + 1)
                if not (isinstance(b, int) and b == 0):
                    act.wait_ge(clo_ready, b)
                slot = ring[0]
                for kd in range(KD):
                    last = A.activation(h32[:, kd], slot[:, kd], ACT.Identity, bias=gb[:, 1, kd:kd + 1], scale=gb[:, 0, kd:kd + 1])
                    if kd == 0:
                        last.then_inc(h32_ready, 1)
                    else:
                        last.then_inc(ring_read, 1)
                act.wait_ge(ring_read, n + 1)
                act.wait_ge(h32_ready, b + 1)
                A.copy(hs[:, 0], h32[:]).then_inc(hhi_ready, 1)

            def latent(b, n, last_use):
                act.wait_ge(ring_full, n + 1)
                act.wait_ge(hlo_ready, b + 1)
                A.copy(h32[:], ring[1][:]).then_inc(ring_read, 1)
                act.wait_ge(ring_read, n + 1)
                if last_use is not None:
                    act.wait_ge(x_full, last_use)
                A.copy(cl[:, 0], h32[:]).then_inc(chi_ready, 1)

            def rounded(g, p, head, ring_done):
                par, s = p % 2, slice(head * DH, (head + 1) * DH)
                o = slice((1 - head) * DH, (2 - head) * DH)
                if head == 0:
                    act.wait_ge(qr_ready, g + 1)
                    if ring_done is not None:
                        act.wait_ge(ring_full, ring_done)
                A.copy(qC[s, par, head], qr[s])
                A.copy(qC[o, par, head], qr[s])
                if head == 0:
                    act.wait_ge(kr_ready, g + 1)
                A.copy(kA[s, par, head], kr[s]).then_inc(hi_ready, 1)

            def rounded_k(p):
                par = p % 2
                for head in range(2):
                    last = A.copy(kB[0:DH, par, head], kr[head * DH:(head + 1) * DH])
                last.then_inc(kb_ready, 1)

            def exps(b, g, p, kt):
                n = ring_at(b, "S", p, kt)
                act.wait_ge(ring_full, n + 1)
                if kt == 0:
                    act.wait_ge(pv_full, g - 1 + PV0)
                    act.wait_ge(summed, 3 * g - 3 + SUM0)
                A.activation(probs[:, p % 2, kt], ring[ring_local(b, "S", p, kt) % 2][:], ACT.Exp, scale=SCALE).then_inc(ring_read, 1)

            def body(i, odd, last_two):
                b, last = 2 * i + odd, last_two and odd == 1
                xs = x_uses(i, odd, last_two)
                for kt in range(TQ):
                    n = ring_at(b, "V", 0, kt)
                    act.wait_ge(ring_full, n + 1)
                    if kt == 0:
                        act.wait_ge(pv_full, PAIRS * b + PV0)
                    A.copy(V[:, kt].rearrange("p (n s) -> p n s", n=2), ring[kt % 2][:]).then_inc(ring_read, 1)
                for p in range(PAIRS):
                    g = PAIRS * b + p
                    nxt = not last or p + 1 < PAIRS
                    done = ring_at(b, "V") if p == 0 else ring_at(b, "S", p - 1, TQ - 1) + 1
                    if nxt:
                        rounded(g + 1, p + 1, 0, done)
                    exps(b, g, p, 0)
                    if nxt:
                        rounded(g + 1, p + 1, 1, None)
                    exps(b, g, p, 1)
                    if nxt:
                        rounded_k(p + 1)
                    exps(b, g, p, 2)
                    exps(b, g, p, 3)
                    if p == 4 and not last:
                        normed(b + 1, ring_at(b, "z"))
                    if p == 5 and not last:
                        latent(b + 1, ring_at(b, "c"), x_at(xs, ("kB", PAIRS - 1)) + 1)

            act.wait_ge(start, 1)
            normed(0, 0)
            latent(0, 1, None)
            rounded(0, 0, 0, None)
            rounded(0, 0, 1, None)
            rounded_k(0)
            each_pair(act, body)

        @block.vector
        def _(dve):
            V_ = nc.vector

            steps, first_step = [0], [0]
            neg, K, thr = one[:, 0:1], one[:, 1:2], cur[:, 0:1]

            def link(ins):
                ins.then_inc(rt_step, 1)
                steps[0] += 1
                dve.wait_ge(rt_step, first_step[0] + steps[0])

            def route_sign(e):
                s = t["scores"][:, bass.ds(e, 1), :].rearrange("p o t -> p (o t)")
                link(V_.tensor_tensor(v[:], s, avail[:], ALU.mult))
                link(V_.tensor_tensor(v[:], v[:], pen[:], ALU.add))
                link(V_.tensor_scalar(w[:, 0], v[:], 0.0, None, ALU.is_ge, ALU.add, accum_out=cnt[:, 0:1]))
                dve.sem_inc(rt_count, 1)

            def route_begin(e):
                s = t["scores"][:, bass.ds(e, 1), :].rearrange("p o t -> p (o t)")
                dve.wait_ge(rt_total, SUMS * e + 1)
                link(V_.tensor_scalar(neg, tot[:, 0:1], float(C), None, ALU.is_lt))
                link(V_.tensor_scalar(one[:, 2:3], neg, -2.0, 1.0, ALU.mult, ALU.add))
                link(V_.tensor_scalar(one[:, 3:4], nrem[:, 0:1], 1.0 - 2.0 * C, None, ALU.add))
                link(V_.tensor_tensor(one[:, 4:5], one[:, 3:4], neg, ALU.mult))
                link(V_.tensor_scalar(K, one[:, 4:5], float(C), None, ALU.add))
                link(V_.tensor_scalar(w[:, 0], s, one[:, 2:3], None, ALU.mult))
                link(V_.tensor_tensor(w[:, 1], w[:, 0], avail[:], ALU.mult))
                link(V_.tensor_tensor(v[:], w[:, 1], pen[:], ALU.add))
                link(V_.memset(cur[:], 0))

            def route_ask(r):
                link(V_.tensor_tensor(cand[:], t["cand_bits"][:, r], cur[:, 0:1].broadcast_to([P, CANDS]), ALU.bitwise_or))
                link(V_.tensor_tensor(ge[:], v[:].unsqueeze(1).broadcast_to([P, CANDS, NT]),
                                      cand[:].bitcast(F32).unsqueeze(2).broadcast_to([P, CANDS, NT]), ALU.is_ge))
                link(V_.tensor_reduce(cnt[:], ge[:], AX.X, ALU.add))
                dve.sem_inc(rt_count, 1)

            def route_take(e, r):
                dve.wait_ge(rt_total, SUMS * e + r + 2)
                width = 1 if r == ROUNDS - 1 else CANDS
                link(V_.tensor_scalar(flags[:, 0:width], tot[:, 0:width], K, None, ALU.is_ge, ALU.add, accum_out=one[:, 5:6]))
                link(V_.tensor_scalar(step[:], one[:, 5:6], float(1 << SHIFTS[r]), None, ALU.mult))
                link(V_.tensor_tensor(cur[:, 0:1], cur[:, 0:1], step[:], ALU.bitwise_or))

            def route_lists():
                thrf = thr.bitcast(F32)
                link(V_.tensor_scalar(w[:, 8], v[:], thrf, None, ALU.is_equal))
                dve.sem_inc(rt_list, 1)
                link(V_.tensor_scalar(w[:, 1], v[:], thrf, None, ALU.is_ge))
                link(V_.tensor_tensor(w[:, 2], w[:, 1], w[:, 8], ALU.subtract))
                link(V_.tensor_tensor(w[:, 3], avail[:], w[:, 1], ALU.subtract))
                link(V_.tensor_tensor(w[:, 3], w[:, 3], w[:, 2], ALU.subtract))
                link(V_.tensor_scalar(w[:, 3], w[:, 3], neg, None, ALU.mult))
                link(V_.tensor_tensor(w[:, 4], w[:, 3], w[:, 2], ALU.add))
                link(V_.reduce_sum(cnt[:, 0:1], w[:, 4], AX.X))
                dve.sem_inc(rt_count, 1)

            def prefix(xs, j):
                n = x_at(xs, ("list", j))
                dve.wait_ge(x_full, n + 1)
                V_.tensor_copy(w[:, 6:8], xb[:, 0:2 * NT].rearrange("p (k t) -> p k t", k=2)).then_inc(x_read, 1)
                dve.wait_ge(x_read, n + 1)
                link(V_.tensor_tensor_scan(w[:, 5], w[:, 7], w[:, 7], 0.0, ALU.add, ALU.bypass))
                link(V_.tensor_tensor(w[:, 5], w[:, 5], w[:, 7], ALU.subtract))
                link(V_.tensor_tensor(w[:, 5], w[:, 5], w[:, 6], ALU.add))

            def route_choose(e, xs):
                dve.wait_ge(rt_total, SUMS * e + SUMS)
                link(V_.tensor_scalar(one[:, 6:7], tot[:, 0:1], -1.0, float(C), ALU.mult, ALU.add))
                prefix(xs, 0)
                link(V_.tensor_scalar(w[:, 5], w[:, 5], one[:, 6:7], None, ALU.is_lt))
                link(V_.tensor_tensor(w[:, 5], w[:, 5], w[:, 8], ALU.mult))
                link(V_.tensor_tensor(w[:, 9], w[:, 5], w[:, 4], ALU.add))
                dve.sem_inc(rt_list, 1)

            def route_place(xs):
                prefix(xs, 1)
                link(V_.tensor_scalar(w[:, 5], w[:, 5], nrem[:, 1:2], None, ALU.add))
                link(V_.tensor_tensor(w[:, 5], w[:, 5], w[:, 9], ALU.mult))
                link(V_.tensor_tensor(pos[:], pos[:], w[:, 5], ALU.add))

            def route_remove():
                link(V_.tensor_tensor(avail[:], avail[:], w[:, 9], ALU.subtract))
                link(V_.tensor_scalar(pen[:], avail[:], -BIG, BIG, ALU.mult, ALU.add))
                link(V_.tensor_scalar(nrem[:, 0:1], nrem[:, 0:1], -float(C), None, ALU.add))
                link(V_.tensor_scalar(nrem[:, 1:2], nrem[:, 1:2], float(C), None, ALU.add))

            STEPS = 3 + 9 + 6 * ROUNDS + 8 + 1 + 3 + 3 + 3 + 3 + 4

            def route_first(e, xs, last_two, k):
                if last_two:
                    if k == 0:
                        steps[0], first_step[0] = 0, ROUTE0 + STEPS * e
                        link(V_.tensor_copy(w[:, 9], avail[:]))
                        dve.sem_inc(rt_list, 1)
                elif k == 0:
                    steps[0], first_step[0] = 0, ROUTE0 + STEPS * e
                    route_sign(e)
                elif k <= ROUNDS:
                    route_ask(k - 1)
                elif k == ROUNDS + 1:
                    route_lists()

            def route_second(e, xs, last_two, k):
                if last_two:
                    if k == 0:
                        route_place(xs)
                        V_.tensor_copy(posi[:], pos[:]).then_inc(rt_rows, 1)
                elif k == 0:
                    route_begin(e)
                elif k <= ROUNDS:
                    route_take(e, k - 1)
                elif k == ROUNDS + 1:
                    route_choose(e, xs)
                elif k == ROUNDS + 2:
                    route_place(xs)
                    route_remove()
                    assert steps[0] == STEPS, (steps[0], STEPS)

            def k_rest(g, p, head):
                par, s = p % 2, slice(head * DH, (head + 1) * DH)
                o = slice((1 - head) * DH, (2 - head) * DH)
                dve.wait_ge(hi_ready, 2 * g + head + 1)
                V_.tensor_tensor(kA[o, par, head], kr[s], kA[s, par, head].bitcast(F32), ALU.subtract).then_inc(alo_ready, 1)


            def q_rest(g, p):
                V_.tensor_tensor(qD[0:DH, p % 2, 1], qr[DH:P], qC[DH:P, p % 2, 1].bitcast(F32), ALU.subtract).then_inc(qlo_ready, 1)

            def reduce(g, j):
                dve.wait_ge(m_full, 4 * g + j + 1)
                V_.tensor_reduce(mx[:, 2 * j:2 * j + 2], mb[:], AX.X, ALU.max, negate=True).then_inc(m_read, 1)

            def rotate(n, what, g):
                dve.wait_ge(x_full, n + 1)
                q = what[0] == "q"
                if what[1] == "A" and not (isinstance(g, int) and g == 0):
                    dve.wait_ge(qr_ready if q else kr_ready, g)
                V_.tensor_tensor(rot[:, (0 if q else 2) + (what[1] == "B")], xb[:], (sin if what[1] == "B" else cos)[:],
                                 ALU.mult).then_inc(x_read, 1)

            def row_maxima(g, p):
                dve.wait_ge(mt_full, g + 1)
                par = p % 2
                V_.tensor_tensor(qD[DH:DH + MROWS, par].rearrange("r h (t n) -> r (h t) n", t=TQ),
                                 mb[0:MROWS, 0, 0:P].unsqueeze(1).broadcast_to([MROWS, MROWS, P]),
                                 own[:].unsqueeze(2).broadcast_to([MROWS, MROWS, P]), ALU.mult).then_inc(m_rows, 1)

            def den_rows(xs, g, p):
                dve.wait_ge(x_full, x_at(xs, ("den", p)) + 1)
                V_.transpose(den_t[:], xb[:]).then_inc(x_read, 1)

            def reciprocals(xs, g, p):
                dve.wait_ge(x_read, x_at(xs, ("den", p)) + 1)
                V_.reciprocal(rec_col[:], den_t[:, ::32]).then_inc(rec_step, 1)
                dve.wait_ge(rec_step, 2 * g + 1)
                V_.transpose(rec[:], rec_col[:].unsqueeze(2).broadcast_to([P, S // 32, 32])).then_inc(rec_step, 1)

            def normalise(b, last, g, p):
                dve.wait_ge(rec_step, 2 * g + 2)
                dve.wait_ge(pv_full, g + 1 + PV0)
                if p == 0:
                    dve.wait_ge(out_full, b + OUT0)
                V_.tensor_tensor(oT[:, p], po[:], rec[:], ALU.mult).then_inc(o_done, 1)

            def body(i, odd, last_two):
                b, last = 2 * i + odd, last_two and odd == 1
                xs = x_uses(i, odd, last_two)
                for p in range(PAIRS):
                    g = PAIRS * b + p
                    ahead = not last or p + 2 < PAIRS
                    nxt = not last or p + 1 < PAIRS

                    def turn(what):
                        if ahead:
                            rotate(x_at(xs, (what, p + 2)), what, g + 2)

                    def red(j):
                        if nxt:
                            reduce(g + 1, j)

                    route_first(i, xs, last_two, PAIRS * odd + p)
                    if nxt:
                        k_rest(g + 1, p + 1, 0)
                    if p:
                        den_rows(xs, g - 1, p - 1)
                    red(0)
                    if nxt:
                        k_rest(g + 1, p + 1, 1)
                    turn("qA")
                    if p:
                        reciprocals(xs, g - 1, p - 1)
                    red(1)
                    turn("qB")
                    if nxt:
                        q_rest(g + 1, p + 1)
                    red(2)
                    turn("kA")
                    red(3)
                    if p:
                        normalise(b, last, g - 1, p - 1)
                    turn("kB")
                    if nxt:
                        row_maxima(g + 1, p + 1)
                    route_second(i, xs, last_two, PAIRS * odd + p)
                g = PAIRS * b + PAIRS - 1
                den_rows(xs, g, PAIRS - 1)
                reciprocals(xs, g, PAIRS - 1)
                normalise(b, last, g, PAIRS - 1)
                dve.wait_ge(out_full, b + 1 + OUT0)
                dve.wait_ge(res_loaded, 16 * b + 16)
                V_.tensor_tensor(zr[:].rearrange("p (i q) d -> p i (q d)", i=2), zr[:].rearrange("p (i q) d -> p i (q d)", i=2),
                                 mb[:], ALU.add).then_inc(out_done, 1)

            for signal, count in ((out_done, OUT0), (out_full, OUT0), (o_done, O0), (pv_full, PV0), (summed, SUM0), (start, 1)):
                dve.sem_inc(signal, count)
            ROUTE0 = 5
            link(V_.memset(avail[:], 1.0))
            link(V_.memset(pen[:], 0.0))
            link(V_.memset(pos[:], 0.0))
            link(V_.memset(nrem[:, 0:1], float(B * S)))
            link(V_.memset(nrem[:, 1:2], 0.0))
            assert steps[0] == ROUTE0
            for par in range(2):
                V_.memset(kB[DH:DH + MROWS, par].bitcast(F32), 1.0)
            for p in range(2):
                for j, what in enumerate(("qA", "qB", "kA", "kB")):
                    rotate(4 * p + j, what, p)
                if p == 0:
                    for head in range(2):
                        k_rest(0, 0, head)
                    q_rest(0, 0)
            for j in range(4):
                reduce(0, j)
            row_maxima(0, 0)
            each_pair(dve, body)

        @block.gpsimd
        def _(pool):
            G = nc.gpsimd

            def rest(dst, src, hi, ready, n, done):
                pool.wait_ge(ready, n)
                G.tensor_tensor(dst, src, hi.bitcast(F32), ALU.subtract).then_inc(done, 1)

            def q_rest(g, p):
                pool.wait_ge(hi_ready, 2 * g + 1)
                G.tensor_tensor(qD[0:DH, p % 2, 0], qr[0:DH], qC[0:DH, p % 2, 0].bitcast(F32), ALU.subtract).then_inc(qlo_ready, 1)

            def sum_q(n, g):
                pool.wait_ge(x_read, n + 1)
                if not (isinstance(g, int) and g == 0):
                    pool.wait_ge(hi_ready, 2 * g)
                    pool.wait_ge(qlo_ready, 2 * g)
                G.tensor_tensor(qr[:], rot[:, 0], rot[:, 1], ALU.add).then_inc(qr_ready, 1)

            def sum_k(n, g):
                pool.wait_ge(x_read, n + 1)
                if not (isinstance(g, int) and g == 0):
                    pool.wait_ge(alo_ready, 2 * g)
                    pool.wait_ge(kb_ready, g)
                G.tensor_tensor(kr[:], rot[:, 2], rot[:, 3], ALU.add).then_inc(kr_ready, 1)

            def sum_partitions(e, j):
                width = CANDS if 1 <= j <= ROUNDS else 1
                pool.wait_ge(rt_count, SUMS * e + j + 1)
                pool.sem_inc(rt_asked, 1)
                G.partition_all_reduce(tot[:, 0:width], cnt[:, 0:width], P, RADD).then_inc(rt_total, 1)

            def scatter_order(columns):
                for j in columns:
                    if j == 0:
                        pool.wait_ge(rt_rows, 1)
                    pool.indirect_dma_start(t["order"], bass.IndirectOffsetOnAxis(ap=posi[:, j:j + 1], axis=0),
                                            t["token_ids"][:, j:j + 1], None).then_inc(rt_scattered, 16)

            def add(b, g, p, kt, free=None):
                pool.wait_ge(ring_read, ring_at(b, "S", p, kt) + 1)
                if kt == 1:
                    pool.wait_ge(x_full, free)
                    src = probs[:, p % 2, 0]
                else:
                    pool.wait_ge(summed, 3 * g + kt - 1 + SUM0)
                    src = psum_k[:]
                G.tensor_tensor(psum_k[:], src, probs[:, p % 2, kt], ALU.add).then_inc(summed, 1)

            def body(i, odd, last_two):
                b, last = 2 * i + odd, last_two and odd == 1
                xs = x_uses(i, odd, last_two)
                for p in range(PAIRS):
                    g = PAIRS * b + p
                    ahead = not last or p + 2 < PAIRS
                    nxt = not last or p + 1 < PAIRS
                    free = xs[0] if p == 0 else x_at(xs, ("den", p - 1)) + 1
                    if nxt:
                        q_rest(g + 1, p + 1)
                    if not last_two and PAIRS * odd + p < SUMS:
                        sum_partitions(i, PAIRS * odd + p)
                    add(b, g, p, 1, free)
                    if ahead:
                        sum_q(x_at(xs, ("qB", p + 2)), g + 2)
                    add(b, g, p, 2)
                    if ahead:
                        sum_k(x_at(xs, ("kB", p + 2)), g + 2)
                    add(b, g, p, 3)
                    if p == 4 and not last:
                        rest(hs[:, 1], h32[:], hs[:, 0], hhi_ready, b + 2, hlo_ready)
                    if p == 5 and not last:
                        rest(cl[:, 1], h32[:], cl[:, 0], chi_ready, b + 2, clo_ready)
                    if last_two:
                        k = PAIRS * odd + p
                        scatter_order(range(NT * (k - 1) // (2 * PAIRS - 1), NT * k // (2 * PAIRS - 1)) if k else ())

            pool.wait_ge(start, 1)
            rest(hs[:, 1], h32[:], hs[:, 0], hhi_ready, 1, hlo_ready)
            rest(cl[:, 1], h32[:], cl[:, 0], chi_ready, 1, clo_ready)
            for p in range(2):
                sum_q(4 * p + 1, p)
                sum_k(4 * p + 3, p)
                if p == 0:
                    q_rest(0, 0)
            each_pair(pool, body)
            pool.wait_ge(rt_scattered, 16 * NT)


def ffn_stage(nc, t, a, B):
    R = F32R
    C = B * S // E
    UT = min(S, C)
    TU = UT // P
    UNITS = C // UT
    CT = C // P
    NB = 2 * UNITS
    AHEAD = NB // 2
    out_rows = t["out"].rearrange("b s d -> (b s) d")
    with ExitStack() as c:
        def sb(name, shape, dt=F32):
            return c.enter_context(nc.sbuf_tensor("ff_" + name, shape, dt))

        def sem(name):
            return c.enter_context(nc.semaphore("ff_" + name))

        raw1 = sb("raw1", [P, KD, FF])
        raw2 = sb("raw2", [P, NF, D])
        w1 = [sb(f"w1_{k}", [P, 2, KD, FF], R) for k in range(2)]
        w2 = [sb(f"w2_{k}", [P, 2, NF, D], R) for k in range(2)]
        idx = [sb(f"idx{k}", [P, CT], I32) for k in range(2)]
        primer = sb("primer", [P, NB], I32)
        b1 = [sb(f"b1_{k}", [P, NF]) for k in range(2)]
        b2 = [sb(f"b2_{k}", [P, D]) for k in range(2)]
        rows = [sb(f"rows{u}", [P, TU, 2 * D]) for u in range(NB)]
        n32 = sb("n32", [P, KD, UT])
        nT = [sb(f"nT{k}", [P, 2, KD, UT], R) for k in range(2)]
        h32 = sb("h32", [P, 2, UT])
        hh = sb("hh", [P, 4, 2, UT], R)
        ps_z = c.enter_context(nc.psum_tensor("ff_ps_z", [P, KD, S], F32))
        ps_h = c.enter_context(nc.psum_tensor("ff_ps_h", [P, 4, S], F32))
        ps_o = c.enter_context(nc.psum_tensor("ff_ps_o", [P, 2, S], F32))

        w_loaded = sem("w_loaded")
        w_rounded, w_split = sem("w_rounded"), sem("w_split")
        small = [sem(f"small{k}") for k in range(2)]
        gathered = [sem(f"gathered{u}") for u in range(NB)]
        scattered = [sem(f"scattered{u}") for u in range(NB)]
        z_full, z_read, n_hi, n_lo = sem("z_full"), sem("z_read"), sem("n_hi"), sem("n_lo")
        up_full, gelu_done, h_hi, h_lo, down_done = [sem(x) for x in ("up_full", "gelu_done", "h_hi", "h_lo", "down_done")]
        gather_begun, scatter_begun, reload = sem("gather_begun"), sem("scatter_begun"), sem("reload")
        n32_half, biased, added = sem("n32_half"), sem("biased"), sem("added")
        G0, L0, H0, A0, SC0 = 4, 2, 4, 1, 16

        def acc(q):
            return ps_o[:, q // 2, (q % 2) * D:(q % 2 + 1) * D]

        block = c.enter_context(nc.Block())

        def each(engine_loop, body):
            if E // 2 > 1:
                with engine_loop(0, E // 2 - 1) as i:
                    body(i, False)
            body(E // 2 - 1, True)

        @block.sync
        def _(sp):
            def load(e, k, expert):
                load_small(k, expert)
                sp.dma_start(raw1[:], a["w1"][expert].rearrange("(k p) f -> p k f", p=P)).then_inc(w_loaded, 16)
                sp.dma_start(raw2[:], a["w2"][expert].rearrange("(n p) d -> p n d", p=P)).then_inc(w_loaded, 16)

            def load_small(k, expert):
                src = t["order"].rearrange("(e t p) o -> e p (t o)", p=P, e=E)[expert]
                sp.dma_start(idx[k][:], src, allow_slow_non_contiguous=True).then_inc(small[k], 16)
                sp.dma_start(b1[k][:], a["b1"][expert]).then_inc(small[k], 16)
                sp.dma_start(b2[k][:], a["b2"][expert].unsqueeze(0).broadcast_to([P, D])).then_inc(small[k], 16)

            def body(i, last):
                for k in range(2):
                    if last and k == 1:
                        break
                    e = 2 * i + k
                    sp.wait_ge(w_split, 2 * (e + 1))
                    sp.sem_inc(reload, 1)
                    for u in range(UNITS * (1 - k), UNITS * (2 - k)):
                        sp.wait_ge(scattered[u], 16 * TU * (i + k) + SC0)
                        sp.sem_inc(reload, 1)
                    load(e, 1 - k, e + 1)

            load(0, 0, 0)
            sp.sem_inc(added, A0)
            sp.sem_inc(gelu_done, G0)
            sp.sem_inc(down_done, H0)
            each(sp.Fori, body)

        @block.gpsimd
        def _(pool):
            G = nc.gpsimd

            def gather(i, u, fresh=False):
                i, u = i + u // NB, u % NB
                k, first = u // UNITS, (u % UNITS) * TU
                if not fresh:
                    pool.wait_ge(scattered[u], 16 * TU * i + SC0)
                if u % UNITS == 0:
                    pool.wait_ge(small[k], 48 * (i + 1))
                pool.sem_inc(gather_begun, 1)
                for q in range(TU):
                    G.indirect_dma_start(rows[u][:, q], None, t["rows"],
                                         bass.IndirectOffsetOnAxis(ap=idx[k][:, first + q:first + q + 1], axis=0)
                                         ).then_inc(gathered[u], 16)

            def scatter(i, u):
                k, first = u // UNITS, (u % UNITS) * TU
                pool.wait_ge(added, NB * i + u + 1 + A0)
                pool.sem_inc(scatter_begun, 1)
                for q in range(TU):
                    G.indirect_dma_start(out_rows, bass.IndirectOffsetOnAxis(ap=idx[k][:, first + q:first + q + 1], axis=0),
                                         rows[u][:, q, D:2 * D], None).then_inc(scattered[u], 16)

            def bias(i, u):
                k = u // UNITS
                pool.wait_ge(gathered[u], 16 * TU * (i + 1))
                pool.wait_ge(small[k], 48 * (i + 1))
                G.tensor_tensor(rows[u][:, :, D:2 * D], rows[u][:, :, D:2 * D],
                                b2[k][:].unsqueeze(1).broadcast_to([P, TU, D]), ALU.add).then_inc(biased, 1)

            def rest(i, u):
                n = NB * i + u
                pool.wait_ge(n_hi, n + 1)
                par = u % 2
                G.tensor_tensor(nT[par][:, 1], n32[:], nT[par][:, 0].bitcast(F32), ALU.subtract).then_inc(n_lo, 1)

            def body(i, last):
                for u in range(NB):
                    end = last and u == NB - 1
                    if not (last and u + AHEAD >= NB):
                        gather(i, u + AHEAD)
                    bias(i, u)
                    if not end:
                        rest(i, u + 1)
                    scatter(i, u)

            for u in range(AHEAD):
                gather(0, u, fresh=True)
            for u in range(NB):
                pool.dma_start(primer[:, u:u + 1], t["order"][0:P]).then_inc(scattered[u], 16)
            rest(0, 0)
            each(pool.Fori, body)
            for u in range(NB):
                pool.wait_ge(scattered[u], 16 * TU * (E // 2) + SC0)

        @block.tensor
        def _(pe):
            T = nc.tensor

            def transposed(i, u):
                n = NB * i + u
                i, u = i + u // NB, u % NB
                pe.wait_ge(gathered[u], 16 * TU * (i + 1))
                if not (isinstance(n, int) and n == 0):
                    pe.wait_ge(z_read, n)
                for kd in range(KD):
                    for q in range(TU):
                        last = T.transpose(ps_z[:, kd, q * P:(q + 1) * P], rows[u][:, q, kd * P:(kd + 1) * P], t["ident"][:])
                last.then_inc(z_full, 1)

            def up(i, u, f):
                k, par = u // UNITS, u % 2
                n = NF * (NB * i + u) + f
                if f == 0:
                    pe.wait_ge(n_lo, NB * i + u + 1)
                    pe.wait_ge(w_split, 2 * (2 * i + k) + 2)
                pe.wait_ge(gelu_done, n - 3 + G0)
                dst = ps_h[:, f % 4, 0:UT]
                for kd in range(KD):
                    wt = [w1[k][:, j, kd, f * P:(f + 1) * P] for j in range(2)]
                    x = [nT[par][:, j, kd] for j in range(2)]
                    T.matmul(dst, wt[0], x[0], start=(kd == 0), stop=False)
                    T.matmul(dst, wt[0], x[1], start=False, stop=False)
                    last = T.matmul(dst, wt[1], x[0], start=False, stop=(kd == KD - 1))
                last.then_inc(up_full, 1)

            def down(i, u, f):
                k = u // UNITS
                n = NF * (NB * i + u) + f
                pe.wait_ge(h_lo, n + 1 + L0)
                if f == 0:
                    pe.wait_ge(added, NB * i + u + A0)
                for q in range(TU):
                    x = [hh[:, f % 4, j, q * P:(q + 1) * P] for j in range(2)]
                    wt = [w2[k][:, j, f] for j in range(2)]
                    for m, (xx, ww) in enumerate(((x[0], wt[0]), (x[0], wt[1]), (x[1], wt[0]))):
                        last = T.matmul(acc(q), xx, ww, start=(f == 0 and m == 0 and q % 2 == 0),
                                        stop=(f == NF - 1 and m == 2), skip_group_check=True)
                last.then_inc(down_done, 1)

            def body(i, last):
                for u in range(NB):
                    for f in range(NF):
                        up(i, u, f)
                        if f >= 2:
                            down(i, u, f - 2)
                        if f == 4 and not (last and u == NB - 1):
                            transposed(i, u + 1)
                    down(i, u, NF - 2)
                    down(i, u, NF - 1)

            transposed(0, 0)
            each(pe.Fori, body)

        @block.scalar
        def _(act):
            A = nc.scalar

            def normed(i, u):
                n = NB * i + u
                par = u % 2
                act.wait_ge(z_full, n + 1)
                if not (isinstance(n, int) and n == 0):
                    act.wait_ge(n_lo, n)
                for kd in range(KD):
                    last = A.activation(n32[:, kd], ps_z[:, kd, 0:UT], ACT.Identity, bias=t["ffn_b"][:, kd:kd + 1],
                                        scale=t["ffn_g"][:, kd:kd + 1])
                    last.then_inc(z_read if kd else n32_half, 1)
                act.wait_ge(n32_half, n + 1)
                act.wait_ge(z_read, n + 1)
                A.copy(nT[par][:, 0], n32[:]).then_inc(n_hi, 1)

            def body(i, last):
                for u in range(NB):
                    k = u // UNITS
                    for f in range(NF):
                        n = NF * (NB * i + u) + f
                        act.wait_ge(up_full, n + 1)
                        if f == 0 and u % UNITS == 0:
                            act.wait_ge(small[k], 48 * (i + 1))
                        act.wait_ge(h_lo, n - 1 + L0)
                        A.activation(h32[:, f % 2], ps_h[:, f % 4, 0:UT], ACT.Gelu_apprx_tanh,
                                     bias=b1[k][:, f:f + 1]).then_inc(gelu_done, 1)
                        if f == 4 and not (last and u == NB - 1):
                            normed(i, u + 1)

            normed(0, 0)
            each(act.Fori, body)

        @block.vector
        def _(dve):
            V = nc.vector

            def convert(e, k, part):
                dst, src = ((w1, raw1), (w2, raw2))[part // 2]
                if part == 0:
                    dve.wait_ge(w_loaded, 32 * (e + 1))
                if part % 2 == 0:
                    V.tensor_copy(dst[k][:, 0], src[:]).then_inc(w_rounded, 1)
                else:
                    dve.wait_ge(w_rounded, 2 * e + part // 2 + 1)
                    V.tensor_tensor(dst[k][:, 1], src[:], dst[k][:, 0].bitcast(F32), ALU.subtract).then_inc(w_split, 1)

            def body(i, last):
                for u in range(NB):
                    k = u // UNITS
                    for f in range(NF):
                        n = NF * (NB * i + u) + f
                        dve.wait_ge(gelu_done, n + 1 + G0)
                        dve.wait_ge(down_done, n - 3 + H0)
                        V.tensor_copy(hh[:, f % 4, 0], h32[:, f % 2]).then_inc(h_hi, 1)
                        dve.wait_ge(h_hi, n + 1)
                        V.tensor_tensor(hh[:, f % 4, 1], h32[:, f % 2], hh[:, f % 4, 0].bitcast(F32),
                                        ALU.subtract).then_inc(h_lo, 1)
                        if u % UNITS == UNITS - 1 and 3 <= f <= 6 and not (last and k == 1):
                            dve.wait_ge(added, NB * i + u + A0)
                            convert(2 * i + k + 1, 1 - k, f - 3)
                    dve.wait_ge(down_done, NF * (NB * i + u + 1) + H0)
                    dve.wait_ge(biased, NB * i + u + 1)
                    if TU == 4:
                        o = rows[u][:, :, D:2 * D]
                        last_add = V.tensor_tensor(o, ps_o[:].rearrange("p i (q d) -> p (i q) d", q=2), o, ALU.add)
                    else:
                        for q in range(TU):
                            o = rows[u][:, q, D:2 * D]
                            last_add = V.tensor_tensor(o, acc(q), o, ALU.add)
                    last_add.then_inc(added, 1)

            dve.sem_inc(h_lo, L0)
            for part in range(4):
                convert(0, 0, part)
            each(dve.Fori, body)


def build(nc, B, a, out):
    T = B * S
    NT = T // P
    rows = nc.dram_tensor("rows_scratch", (T, 2 * D), F32).ap()
    order = nc.dram_tensor("order_scratch", (T, 1), I32).ap()
    with ExitStack() as c:
        def sb(name, shape, dt=F32):
            return c.enter_context(nc.sbuf_tensor(name, shape, dt))

        t = {
            "x": a["x"],
            "rows": rows,
            "rows_by_seq": rows.rearrange("(b t p) c -> b p t c", p=P, t=TQ),
            "order": order,
            "out": out,
            "ident": sb("ident", [P, P]),
            "ones": sb("ones", [P, P]),
            "ffn_g": sb("ffn_g", [P, KD]),
            "ffn_b": sb("ffn_b", [P, KD]),
        }
        attention_stack = c.enter_context(ExitStack())
        for name, shape, dt in (
            ("wq", [P, 2, 2, H * DH], F32R),
            ("wk", [P, 2, 2, H * DH], F32R),
            ("wv", [P, 2, H * DH], F32R),
            ("wd", [P, 2, KD, 2, L], F32R),
            ("wo", [P, PAIRS, D], F32), ("cos", [P, S], F32), ("sin", [P, S], F32),
            ("own", [MROWS, MROWS], F32), ("gb", [P, 2, KD], F32),
        ):
            t[name] = attention_stack.enter_context(nc.sbuf_tensor("at_" + name, shape, dt))
        scores_stack = c.enter_context(ExitStack())

        def sc(name, shape, dt=F32):
            return scores_stack.enter_context(nc.sbuf_tensor(name, shape, dt))

        t["scores"] = sc("scores", [P, E, NT])
        t["centT"] = sc("centT", [P, KD, E])
        t["before"] = sc("before", [P, P])
        t["token_ids"] = sc("token_ids", [P, NT], I32)
        t["cand_bits"] = sc("cand_bits", [P, len(SHIFTS), CANDS], I32)
        loaded = c.enter_context(nc.semaphore("consts_loaded"))
        with nc.Block() as block:
            @block.sync
            def _(sp):
                loads = [
                    (t["ident"][:], a["ident"]),
                    (t["before"][:], a["before"]),
                    (t["ones"][:], a["ones"]),
                    (t["ffn_g"][:], a["ffn_g"]),
                    (t["ffn_b"][:], a["ffn_b"]),
                    (t["centT"][:], a["centT"].rearrange("(k p) e -> p k e", p=P)),
                    (t["token_ids"][:], a["token_ids"]),
                    (t["cand_bits"][:], a["cand_bits"]),
                ]
                for dst, src in loads:
                    sp.dma_start(dst, src).then_inc(loaded, 16)
                sp.wait_ge(loaded, 16 * len(loads))
        layer_norm_stage(nc, t, a, B)
        attention_stage(nc, t, a, B)
        scores_stack.close()
        attention_stack.close()
        ffn_stage(nc, t, a, B)


def constants(B):
    NT = B * S // P
    p = np.arange(P)
    rounds = np.array([[c << s if (c << s) < 2**31 else 0 for c in range(1, CANDS + 1)] for s in SHIFTS], np.int64).astype(np.int32)
    inv_freq = 1.0 / 10000.0 ** (np.arange(0, DH, 2, dtype=np.float32) / DH)
    freqs = np.outer(np.arange(S, dtype=np.float32), inv_freq)
    cos = np.concatenate([np.cos(freqs), np.cos(freqs)], -1)[:, ::2]
    sin = np.concatenate([np.sin(freqs), np.sin(freqs)], -1)[:, ::2]
    pair = (p % DH) // 2
    sign = np.where(p % 2 == 0, -1.0, 1.0).astype(np.float32)
    head_tile = np.arange(MROWS)
    return {
        "ident": np.eye(P, dtype=np.float32),
        "before": (p[:, None] < p[None, :]).astype(np.float32),
        "ones": np.ones((P, P), np.float32),
        "token_ids": (np.arange(NT)[None, :] * P + p[:, None]).astype(np.int32),
        "cand_bits": np.broadcast_to(rounds, (P, len(SHIFTS), CANDS)).copy(),
        "cos": np.ascontiguousarray(cos[:, pair].T.astype(np.float32)),
        "sin": np.ascontiguousarray((sin[:, pair].T * sign[:, None]).astype(np.float32)),
        "own_tile": np.ascontiguousarray(np.eye(MROWS, dtype=np.float32)),
    }


def arrays_of(inputs):
    i = {k: np.asarray(v) for k, v in inputs.items()}
    cc = np.ascontiguousarray
    B = i["L0_attn_x"].shape[0]

    def columns(v):
        return cc(v.reshape(-1, P).T)

    swap = np.arange(H * DH).reshape(-1, 2)[:, ::-1].ravel()
    return {
        "x": cc(i["L0_attn_x"]),
        "wdqT": cc(i["L0_attn_w_down_q"].T), "wdkvT": cc(i["L0_attn_w_down_kv"].T),
        "wq": cc(np.stack([i["L0_attn_w_up_q"].T, i["L0_attn_w_up_q"][swap].T], 1)),
        "wk": cc(np.stack([i["L0_attn_w_up_k"].T, i["L0_attn_w_up_k"][swap].T], 1)),
        "wv": cc(i["L0_attn_w_up_v"].T), "woT": cc(i["L0_attn_w_out"].T),
        "attn_g": columns(i["L0_attn_ln_scale"]), "attn_b": columns(i["L0_attn_ln_bias"]),
        "centT": cc(i["L0_ffn_centroids"].T), "ffn_g": columns(i["L0_ffn_ln_g"]), "ffn_b": columns(i["L0_ffn_ln_b"]),
        "w1": cc(i["L0_ffn_w1"]), "b1": cc(i["L0_ffn_b1"].reshape(E, NF, P).transpose(0, 2, 1)), "w2": cc(i["L0_ffn_w2"]), "b2": cc(i["L0_ffn_b2"]),
        **constants(B),
    }


def kernel(**inputs):
    import concourse.bacc as bacc
    from concourse.bass_utils import run_bass_kernel_spmd

    arrays = arrays_of(inputs)
    B = arrays["x"].shape[0]
    nc = bacc.Bacc("TRN2", target_bir_lowering=False, num_devices=1)
    a = {n: nc.dram_tensor("in_" + n, v.shape, mybir.dt.from_np(v.dtype), kind="ExternalInput").ap() for n, v in arrays.items()}
    out = nc.dram_tensor("out", (B, S, D), F32, kind="ExternalOutput").ap()
    build(nc, B, a, out)
    got = run_bass_kernel_spmd(nc, [{"in_" + n: v for n, v in arrays.items()}], core_ids=[0])
    return got.results[0]["out"]
```
